# Optimizing a Trainium2 kernel written in Bass

```python
import numpy as np
import jax
import jax.numpy as jnp

def _softmax(x, axis=-1):
    return jax.nn.softmax(x, axis=axis)

def _gelu(x):
    return jax.nn.gelu(x, approximate=True)

def _silu(x):
    return jax.nn.silu(x)

def _sigmoid(x):
    return jax.nn.sigmoid(x)

def _layernorm(x, axis=-1, eps=1e-05):
    m = jnp.mean(x, axis=axis, keepdims=True)
    v = jnp.var(x, axis=axis, keepdims=True)
    return (x - m) / jnp.sqrt(v + eps)

def _scatter_add(tgt, idx, src, axis=0):
    return tgt.at[idx].add(src)

def _segment_sum(src, seg, n):
    return jax.ops.segment_sum(src, seg, n)
kernel_name = 'mk_gnn_preln_d2_gnn_r8_8cc54d'

def setup_inputs(seed: int=0):
    np.random.seed(seed)
    _w = jnp.asarray

    def _rec_inputs():
        import jax
        import jax.numpy as jnp
        _gk = jax.random.key(seed)
        x = -0.000202 + 1 * jax.random.normal(jax.random.fold_in(_gk, 1), (12500, 64), jnp.float32)
        _s = jax.random.randint(jax.random.fold_in(_gk, 2), (100000,), 0, 12500, jnp.int32)
        _d = jax.random.randint(jax.random.fold_in(_gk, 3), (100000,), 0, 12500, jnp.int32)
        _loop = jnp.arange(12500, dtype=jnp.int32)
        src = jnp.concatenate([_s, _d, _loop])
        dst = jnp.concatenate([_d, _s, _loop])
        _o = jnp.argsort(dst, stable=True)
        src = src[_o]
        dst = dst[_o]
        edge_attr_64 = -8.16379e-05 + 0.999858 * jax.random.normal(jax.random.fold_in(_gk, 12), (212500, 64), jnp.float32)
        return (x, src, dst, edge_attr_64)
    x, src, dst, edge_attr_64 = _rec_inputs()

    def _L0_gnn_setup():
        import jax, jax.numpy as jnp
        import numpy as np
        N_NODES = 12500
        N_EDGES = 200000
        EMB = 64
        BN_EPS = 1e-05
        key = jax.random.key(seed)
        ks = jax.random.split(key, 8)
        node_feats = jax.random.normal(ks[0], (N_NODES, EMB), dtype=jnp.float32)
        edge_feats = jax.random.normal(ks[1], (N_EDGES, EMB), dtype=jnp.float32)
        src = jax.random.randint(ks[2], (N_EDGES,), 0, N_NODES, dtype=jnp.int32)
        dst = jax.random.randint(ks[3], (N_EDGES,), 0, N_NODES, dtype=jnp.int32)
        lim1 = 1.0 / np.sqrt(EMB)
        lim2 = 1.0 / np.sqrt(2 * EMB)
        W1 = jax.random.uniform(ks[4], (EMB, 2 * EMB), minval=-lim1, maxval=lim1, dtype=jnp.float32)
        b1 = jax.random.uniform(ks[5], (2 * EMB,), minval=-lim1, maxval=lim1, dtype=jnp.float32)
        W2 = jax.random.uniform(ks[6], (2 * EMB, EMB), minval=-lim2, maxval=lim2, dtype=jnp.float32)
        b2 = jax.random.uniform(ks[7], (EMB,), minval=-lim2, maxval=lim2, dtype=jnp.float32)
        bn_gamma = jnp.ones((EMB,), dtype=jnp.float32)
        bn_beta = jnp.zeros((EMB,), dtype=jnp.float32)
        return {'node_feats': node_feats, 'edge_feats': edge_feats, 'src': src, 'dst': dst, 'W1': W1, 'b1': b1, 'W2': W2, 'b2': b2, 'bn_gamma': bn_gamma, 'bn_beta': bn_beta}
    _L0_gnn_all = _L0_gnn_setup()
    _L0_gnn_in = {k: v for k, v in _L0_gnn_all.items() if k in ('W1', 'b1', 'W2', 'b2', 'bn_gamma', 'bn_beta')}
    del _L0_gnn_all

    def _L1_gnn_setup():
        import jax, jax.numpy as jnp
        import numpy as np
        N = 12500
        E = 200000
        IN_C = 64
        HID_C = 64
        OUT_C = 64
        GW = 0.8
        EPS = 1e-05

        def _gcn_conv(x, W, b, src, dst, enorm, n):
            xw = x @ W
            msg = xw[src] * enorm[:, None]
            out = jax.ops.segment_sum(msg, dst, num_segments=n)
            return out + b
        key = jax.random.key(seed)
        ks = jax.random.split(key, 8)
        node_features = jax.random.normal(ks[0], (N, IN_C), dtype=jnp.float32)
        edges = jax.random.randint(ks[1], (2, E), 0, N, dtype=jnp.int64)
        s1 = 1.0 / np.sqrt(IN_C)
        s2 = 1.0 / np.sqrt(HID_C)
        W1 = jax.random.uniform(ks[2], (IN_C, HID_C), jnp.float32, -s1, s1)
        b1 = jnp.zeros((HID_C,), jnp.float32)
        W2 = jax.random.uniform(ks[3], (HID_C, OUT_C), jnp.float32, -s2, s2)
        b2 = jnp.zeros((OUT_C,), jnp.float32)
        ln_w = jnp.ones((1,), jnp.float32)
        ln_b = jnp.zeros((1,), jnp.float32)
        return {'node_features': node_features, 'edges': edges, 'W1': W1, 'b1': b1, 'W2': W2, 'b2': b2, 'ln_w': ln_w, 'ln_b': ln_b}
    _L1_gnn_all = _L1_gnn_setup()
    _L1_gnn_in = {k: v for k, v in _L1_gnn_all.items() if k in ('W1', 'b1', 'W2', 'b2', 'ln_w', 'ln_b')}
    del _L1_gnn_all
    return {'x': x, 'src': src, 'dst': dst, 'edge_attr_64': edge_attr_64, 'L0_gnn_W1': _L0_gnn_in['W1'], 'L0_gnn_b1': _L0_gnn_in['b1'], 'L0_gnn_W2': _L0_gnn_in['W2'], 'L0_gnn_b2': _L0_gnn_in['b2'], 'L0_gnn_bn_gamma': _L0_gnn_in['bn_gamma'], 'L0_gnn_bn_beta': _L0_gnn_in['bn_beta'], 'L1_gnn_W1': _L1_gnn_in['W1'], 'L1_gnn_b1': _L1_gnn_in['b1'], 'L1_gnn_W2': _L1_gnn_in['W2'], 'L1_gnn_b2': _L1_gnn_in['b2'], 'L1_gnn_ln_w': _L1_gnn_in['ln_w'], 'L1_gnn_ln_b': _L1_gnn_in['ln_b']}

def reference(x, src, dst, edge_attr_64, L0_gnn_W1, L0_gnn_b1, L0_gnn_W2, L0_gnn_b2, L0_gnn_bn_gamma, L0_gnn_bn_beta, L1_gnn_W1, L1_gnn_b1, L1_gnn_W2, L1_gnn_b2, L1_gnn_ln_w, L1_gnn_ln_b):
    import jax
    import jax.numpy as jnp

    def _L0_gnn_ref(node_feats, edge_feats, src, dst, W1, b1, W2, b2, bn_gamma, bn_beta):
        import jax, jax.numpy as jnp
        import numpy as np
        N_NODES = 12500
        N_EDGES = 200000
        EMB = 64
        BN_EPS = 1e-05
        n_nodes = node_feats.shape[0]
        msg = node_feats[src] + edge_feats
        agg = jax.ops.segment_sum(msg, dst, num_segments=n_nodes)
        h = jax.nn.relu(agg @ W1 + b1) @ W2 + b2
        mean = jnp.mean(h, axis=0)
        var = jnp.mean(jnp.square(h - mean), axis=0)
        h = (h - mean) * jax.lax.rsqrt(var + BN_EPS) * bn_gamma + bn_beta
        return h

    def _L1_gnn_ref(node_features, edges, W1, b1, W2, b2, ln_w, ln_b):
        import jax, jax.numpy as jnp
        import numpy as np
        N = 12500
        E = 200000
        IN_C = 64
        HID_C = 64
        OUT_C = 64
        GW = 0.8
        EPS = 1e-05

        def _gcn_conv(x, W, b, src, dst, enorm, n):
            xw = x @ W
            msg = xw[src] * enorm[:, None]
            out = jax.ops.segment_sum(msg, dst, num_segments=n)
            return out + b
        n = node_features.shape[0]
        loops = jnp.arange(n, dtype=edges.dtype)
        src = jnp.concatenate([edges[0], loops])
        dst = jnp.concatenate([edges[1], loops])
        deg = jax.ops.segment_sum(jnp.ones_like(dst, dtype=node_features.dtype), dst, num_segments=n)
        dis = jnp.where(deg > 0, jax.lax.rsqrt(deg), 0.0)
        enorm = dis[src] * dis[dst]
        h = jax.nn.relu(_gcn_conv(node_features, W1, b1, src, dst, enorm, n))
        x = GW * h + (1.0 - GW) * h
        x = jax.nn.relu(_gcn_conv(x, W2, b2, src, dst, enorm, n))
        mean = jnp.mean(x)
        var = jnp.mean((x - mean) ** 2)
        x = (x - mean) * jax.lax.rsqrt(var + EPS) * ln_w + ln_b
        return x
    edge_index = jnp.stack([src, dst])
    h = jnp.maximum(_layernorm(x, axis=-1), 0.0)
    x = x + _L0_gnn_ref(h, edge_attr_64, src, dst, L0_gnn_W1, L0_gnn_b1, L0_gnn_W2, L0_gnn_b2, L0_gnn_bn_gamma, L0_gnn_bn_beta)
    h = jnp.maximum(_layernorm(x, axis=-1), 0.0)
    x = x + _L1_gnn_ref(h, edge_index, L1_gnn_W1, L1_gnn_b1, L1_gnn_W2, L1_gnn_b2, L1_gnn_ln_w, L1_gnn_ln_b)
    return x

_drawn_inputs = setup_inputs


def setup_inputs(seed=0):
    import zlib

    import numpy as np

    out = dict(_drawn_inputs(seed))
    spreads = {'L0_gnn_bn_gamma': (1.0, 0.2),
     'L0_gnn_bn_beta': (0.0, 0.1),
     'L1_gnn_b1': (0.0, 0.1),
     'L1_gnn_b2': (0.0, 0.1)}
    factors = {'L0_gnn_b1': 6.486, 'L0_gnn_b2': 8.0}
    for name, (base, spread) in spreads.items():
        noise = np.random.default_rng([zlib.crc32(name.encode()), seed]).standard_normal(out[name].shape)
        drawn = base * np.exp(spread * noise) if base else spread * noise
        out[name] = jnp.asarray(drawn.astype(out[name].dtype))
    for name, factor in factors.items():
        out[name] = (out[name] * factor).astype(out[name].dtype)
    return out
```

```python
from contextlib import ExitStack

import concourse.bass as bass
from concourse import mybir

ALU = mybir.AluOpType
ACT = mybir.ActivationFunctionType
F32 = mybir.dt.float32
I32 = mybir.dt.int32
X = mybir.AxisListType.X
ds = bass.ds

P = 128
F = 64
HID = 128
PN = 125
W = 128
NT = 10
NSLOT = 6
NS = 3
NPS = 3
EPS = 1e-05
GW = 0.8


class Sem:

    def __init__(self, handle):
        self.h = handle
        self.n = 0

    def inc(self, ins, by=1):
        ins.then_inc(self.h, by)
        self.n += by
        return (self.h, self.n)


def bass_gnn_preln_kernel(nc, x, src, dst, edge, W01, b01, W02, b02, gamma, beta,
                          W11, b11, W12, b12, ln_w, ln_b, out):
    N = x.shape[0]
    E = src.shape[0]
    J = N // PN
    G = E // (P * NT)
    R = E - G * P * NT
    assert N == J * PN and 1 < R <= P
    NG = G + 1
    JF = J * F

    pe, act, dve, pool, sp = nc.tensor, nc.scalar, nc.vector, nc.gpsimd, nc.sync

    def wait(eng, *points):
        for h, n in points:
            eng.wait_ge(h, n)

    with ExitStack() as ctx:
        def sb(name, shape, dt=F32):
            return ctx.enter_context(nc.sbuf_tensor(name, shape, dt))

        def sem(name):
            return Sem(ctx.enter_context(nc.semaphore(name)))

        def dram(name, shape):
            return nc.dram_tensor(name, shape, F32, kind="Internal").ap()

        tables = [dram(f"table{k}", [N, F]) for k in range(3)]
        deg_dram = dram("deg_dram", [1, N])

        acc = sb("acc", [P, N + W])
        big = sb("big", [P, max(N, NSLOT * 2 * NT * F + NS * NT * W)])
        X1 = sb("X1", [P, JF])
        H = sb("H", [P, JF])
        C = sb("C", [P, JF])
        srcT = sb("srcT", [P, NT, G], I32)
        relT = sb("relT", [P, NT, G])
        src_l = sb("src_l", [P, 1], I32)
        dst_l = sb("dst_l", [P, 1], I32)
        dstb_l = sb("dstb_l", [P, 1], I32)
        rel_l = sb("rel_l", [P, 3])
        base = sb("base", [1, NG], I32)
        iota_i = sb("iota_i", [P, W], I32)
        iota = sb("iota", [P, W])
        rowid = sb("rowid", [P, 1], I32)
        rowf = sb("rowf", [P, 1])
        ident = sb("ident", [P, P])
        ones = sb("ones", [P, P])
        w01 = sb("w01", [F, HID])
        w02 = sb("w02", [HID, F])
        w11 = sb("w11", [F, F])
        w12 = sb("w12", [F, F])
        w12a = sb("w12a", [F, F])
        w12b = sb("w12b", [F, F])
        b01c = sb("b01c", [HID, 1])
        rows = sb("rows", [P, 5, F])
        lnwb = sb("lnwb", [P, 2])
        mean = sb("mean", [P, J])
        var = sb("var", [P, J])
        dis = sb("dis", [P, J])
        st = sb("st", [P, 4, F])
        sc = sb("sc", [P, 8])
        epst = sb("epst", [P, 1])
        mm = sb("mm", [P, 16])
        flag = sb("flag", [1, 1], I32)
        g_src = sb("g_src", [P, NT], I32)
        g_dst = sb("g_dst", [P, NT], I32)
        g_cur = sb("g_cur", [P, NT])

        ps_g = [ctx.enter_context(nc.psum_tensor(f"ps_g{i}", [P, 512], F32)) for i in range(NPS)]
        ps_t = [ctx.enter_context(nc.psum_tensor(f"ps_t{i}", [P, 512], F32)) for i in range(2)]
        ps_h = [ctx.enter_context(nc.psum_tensor(f"ps_h{i}", [P, 512], F32)) for i in range(2)]
        ps_s = ctx.enter_context(nc.psum_tensor("ps_s", [P, 512], F32))

        def gbuf(k):
            return big[:, k * NT * F:(k + 1) * NT * F].rearrange("p (t f) -> p t f", f=F)

        def ebuf(k):
            return gbuf(NSLOT + k)

        def sbuf(k):
            o = NSLOT * 2 * NT * F + k * NT * W
            return big[:, o:o + NT * W].rearrange("p (t w) -> p t w", w=W)

        s_c = sem("s_c")
        s_in = [sem(f"s_in{i}") for i in range(6)]
        s_v = sem("s_v")
        s_a = sem("s_a")
        s_p = sem("s_p")
        s_k = sem("s_k")
        s_tab = sem("s_tab")
        s_deg = sem("s_deg")
        s_out = sem("s_out")
        s_gat = [sem(f"s_gat{i}") for i in range(NSLOT)]
        s_edg = [sem(f"s_edg{i}") for i in range(NSLOT)]
        s_S = sem("s_S")
        s_mm = sem("s_mm")
        s_add = sem("s_add")
        s_pass = sem("s_pass")
        t_src = sem("t_src")
        t_dst = sem("t_dst")
        t_edg = sem("t_edg")
        t_gat = sem("t_gat")
        t_cur = sem("t_cur")
        t_S = sem("t_S")
        t_mm = sem("t_mm")
        t_add = sem("t_add")
        t_end = sem("t_end")

        def V(ins):
            p = s_v.inc(ins)
            wait(dve, p)
            return p

        edge_g = edge[0:G * P * NT, :].rearrange("(g p t) f -> g p t f", p=P, t=NT)
        edge_r = edge[G * P * NT:E, :]
        src_g = src[0:G * P * NT].rearrange("(g p t) -> g p t", p=P, t=NT)
        dst_g = dst[0:G * P * NT].rearrange("(g p t) -> g p t", p=P, t=NT)
        src_r = src[G * P * NT:E].rearrange("(p a) -> p a", a=1)
        dst_r = dst[G * P * NT:E].rearrange("(p a) -> p a", a=1)
        blocks = [(b, min(P, G - b)) for b in range(0, G, P)]
        NB = len(blocks)
        EG = P * NT

        def raw(k, b, r):
            return acc[0:r, (k * NB + b) * EG:(k * NB + b + 1) * EG]

        xv = x.rearrange("(p j) f -> p (j f)", p=PN)
        for k, a in ((0, dst), (1, src)):
            for b, (g0, r) in enumerate(blocks):
                rows_d = a[g0 * EG:(g0 + r) * EG].rearrange("(g e) -> g e", e=EG)
                p_raw = s_in[k].inc(sp.dma_start(raw(k, b, r).bitcast(I32), rows_d), 16)
            if k == 0:
                p_dst = p_raw
            else:
                p_src = p_raw
        NCH = 4
        JC = J // NCH if J % NCH == 0 else J
        NCH = J // JC
        p_x = []
        for c in range(NCH):
            s = s_in[2] if c == 0 else sem(f"s_x{c}")
            p_x.append(s.inc(act.dma_start(X1[0:PN, c * JC * F:(c + 1) * JC * F],
                                           xv[:, c * JC * F:(c + 1) * JC * F]), 16))
        s_in[3].inc(sp.dma_start(base[0:1, 0:G], dst[0:G * EG].rearrange("(g e) -> e g", e=EG)[0:1, :],
                                allow_slow_non_contiguous=True), 16)
        s_in[3].inc(sp.dma_start(base[0:1, G:NG], dst[G * EG:G * EG + 1].rearrange("(a b) -> a b", a=1)), 16)
        s_in[3].inc(sp.dma_start(src_l[0:R, :], src_r), 16)
        s_in[3].inc(sp.dma_start(dst_l[0:R, :], dst_r), 16)
        p_small = s_in[3].inc(sp.dma_start(
            dstb_l[0:R, :], dst[G * EG:G * EG + 1].rearrange("(a b) -> a b", a=1).broadcast_to([R, 1])), 16)
        for t, a in ((w01, W01), (w02, W02), (w11, W11), (w12, W12)):
            s_in[4].inc(sp.dma_start(t[:, :], a), 16)
        s_in[4].inc(sp.dma_start(b01c[:, :], b01.rearrange("(a b) -> a b", b=1)), 16)
        for i, a in enumerate((b02, gamma, beta, b11, b12)):
            s_in[4].inc(sp.dma_start(rows[:, i, :], a.rearrange("(a b) -> a b", a=1).broadcast_to([P, F])), 16)
        for i, a in enumerate((ln_w, ln_b)):
            p_w = s_in[4].inc(sp.dma_start(lnwb[:, i:i + 1], a.rearrange("(a b) -> a b", a=1).broadcast_to([P, 1])), 16)

        p_i0 = s_k.inc(pool.iota(iota_i[:, :], pattern=[[1, W]], base=0, channel_multiplier=0))
        p_i1 = s_k.inc(pool.iota(rowid[:, :], pattern=[[0, 1]], base=0, channel_multiplier=1))
        wait(dve, p_i1)
        V(dve.tensor_copy(iota[:, :], iota_i[:, :]))
        V(dve.tensor_copy(rowf[:, :], rowid[:, :]))
        p_id = V(dve.tensor_scalar(ident[:, :], iota[:, 0:P], rowf[:, 0:1], None, ALU.is_equal))
        V(dve.memset(epst[:, :], EPS))
        V(dve.memset(mm[:, :], 0.0))
        p_ones = V(dve.memset(ones[:, :], 1.0))

        relf = [big[0:r, b * EG:(b + 1) * EG] for b, (g0, r) in enumerate(blocks)]
        srcf = [big[0:r, (NB + b) * EG:(NB + b + 1) * EG] for b, (g0, r) in enumerate(blocks)]
        wait(dve, p_dst)
        for b, (g0, r) in enumerate(blocks):
            V(dve.tensor_copy(relf[b], raw(0, b, r).bitcast(I32)))
            V(dve.tensor_copy(mm[0:r, 15:16], relf[b][:, 0:1]))
            V(dve.tensor_scalar(relf[b], relf[b], mm[0:r, 15:16], None, ALU.subtract))
            V(dve.tensor_reduce(mm[0:r, 4 * b:4 * b + 1], relf[b], X, ALU.max))
            V(dve.tensor_reduce(mm[0:r, 4 * b + 1:4 * b + 2], relf[b], X, ALU.min))
        wait(dve, p_src)
        for b, (g0, r) in enumerate(blocks):
            p_raw2 = V(dve.tensor_copy(srcf[b], raw(1, b, r).bitcast(I32)))
        wait(dve, p_small)
        V(dve.tensor_copy(rel_l[0:R, 0:1], dst_l[0:R, :]))
        V(dve.tensor_copy(rel_l[0:R, 1:2], dstb_l[0:R, :]))
        V(dve.tensor_tensor(rel_l[0:R, 2:3], rel_l[0:R, 0:1], rel_l[0:R, 1:2], ALU.subtract))
        V(dve.tensor_copy(mm[0:R, 12:13], rel_l[0:R, 2:3]))
        V(dve.tensor_copy(mm[0:R, 13:14], rel_l[0:R, 2:3]))
        V(dve.tensor_reduce(mm[:, 14:15], mm[:, 0:14], X, ALU.max))
        V(dve.tensor_reduce(mm[:, 15:16], mm[:, 0:14], X, ALU.min))
        V(dve.tensor_scalar(mm[:, 0:1], mm[:, 14:15], float(W - 1), None, ALU.is_gt))
        V(dve.tensor_scalar(mm[:, 1:2], mm[:, 15:16], 0.0, None, ALU.is_lt))
        p_f = V(dve.tensor_tensor(mm[:, 2:3], mm[:, 0:1], mm[:, 1:2], ALU.add))

        tq = []
        k = 0
        free = {}
        nt_b = 512 // G if G < 512 else 1
        nt_b = min(nt_b, NT)
        for what, mats in (("src", srcf), ("rel", relf)):
            for t0 in range(0, NT, nt_b):
                n = min(nt_b, NT - t0)
                pt = ps_t[k % 2]
                wait(pe, p_raw2, p_id, *([free[k - 2]] if k >= 2 else []))
                for i in range(n):
                    for b, (g0, r) in enumerate(blocks):
                        last = pe.transpose(pt[:, i * G + g0:i * G + g0 + r],
                                            mats[b][:, t0 + i:EG:NT], ident[0:r, 0:r])
                p_t = s_p.inc(last)
                wait(dve, p_t)
                tgt = srcT if what == "src" else relT
                free[k] = V(dve.tensor_copy(tgt[:, t0:t0 + n, :],
                                            pt[:, 0:n * G].rearrange("p (t g) -> p t g", g=G)))
                k += 1
            if what == "src":
                p_srcT = free[k - 1]
        p_relT = free[k - 1]
        wait(pe, p_f, p_ones)
        p_fs = s_p.inc(pe.matmul(ps_s[0:1, 0:1], mm[:, 2:3], ones[:, 0:1], start=True, stop=True))
        wait(dve, p_fs)
        V(dve.tensor_scalar(mm[0:1, 3:4], ps_s[0:1, 0:1], 0.0, None, ALU.is_gt))
        p_flag = V(dve.tensor_copy(flag[:, :], mm[0:1, 3:4]))
        wait(dve, p_t)
        p_zero = V(dve.memset(acc[:, :], 0.0))

        engines = [pe, dve, pool, sp]
        for eng in engines:
            wait(eng, p_flag)
        fv = nc.values_load(flag[0:1, 0:1], engines=[e.engine for e in engines], min_val=0, max_val=1)

        def bc_f(t, j0, j1):
            return t[0:PN, j0:j1].rearrange("p (j a) -> p j a", a=1).broadcast_to([PN, j1 - j0, F])

        def v3(t, j0, j1):
            return t[0:PN, j0 * F:j1 * F].rearrange("p (j f) -> p j f", f=F)

        def norm_table(k, ready, scale):
            done = []
            for c in range(NCH):
                j0, j1 = c * JC, (c + 1) * JC
                wait(dve, ready[c])
                V(dve.tensor_reduce(mean[0:PN, j0:j1], v3(X1, j0, j1), X, ALU.add))
                V(dve.tensor_scalar(mean[0:PN, j0:j1], mean[0:PN, j0:j1], 1.0 / F, None, ALU.mult))
                p = V(dve.tensor_tensor(v3(H, j0, j1), v3(X1, j0, j1), bc_f(mean, j0, j1), ALU.subtract))
                wait(act, p)
                p = s_a.inc(act.activation(C[0:PN, j0 * F:j1 * F], H[0:PN, j0 * F:j1 * F], ACT.Square))
                wait(dve, p)
                p = V(dve.tensor_reduce(var[0:PN, j0:j1], v3(C, j0, j1), X, ALU.add))
                wait(act, p)
                p = s_a.inc(act.activation(var[0:PN, j0:j1], var[0:PN, j0:j1], ACT.Sqrt,
                                           bias=epst[0:PN, 0:1], scale=1.0 / F))
                wait(dve, p)
                V(dve.reciprocal(var[0:PN, j0:j1], var[0:PN, j0:j1]))
                if scale is not None:
                    V(dve.tensor_tensor(var[0:PN, j0:j1], var[0:PN, j0:j1], scale[0:PN, j0:j1], ALU.mult))
                p = V(dve.scalar_tensor_tensor(out=v3(H, j0, j1), in0=v3(H, j0, j1), scalar=0.0,
                                               in1=bc_f(var, j0, j1), op0=ALU.max, op1=ALU.mult))
                wait(sp, p)
                done.append(p)
                s_tab.inc(sp.dma_start(tables[k].rearrange("(p j) f -> p (j f)", p=PN)[:, j0 * F:j1 * F],
                                       H[0:PN, j0 * F:j1 * F]), 16)
            return done

        turn = [0]
        fast_engines = [pe, dve, pool, sp]
        point = {}

        def edge_matmuls(ps, t, parts, S, gb, eb, first, stop):
            if eb is not None:
                pe.matmul(ps[0:F, 0:W], eb[0:parts, t, :], S[0:parts, t, :], start=first, stop=False)
                pe.matmul(ps[F:F + 1, 0:W], ones[0:parts, 0:1], S[0:parts, t, :], start=first, stop=stop)
            return pe.matmul(ps[0:F, 0:W], gb[0:parts, t, :], S[0:parts, t, :],
                             start=first and eb is None, stop=stop)

        def fast_pass(k, acc_ready):
            rows_a = F + 1 if k == 0 else F
            tab = (s_tab.h, s_tab.n)
            wait(pool, p_srcT, p_small, tab)
            wait(pe, p_ones)
            wait(dve, acc_ready)
            pend = None

            def add(pend):
                g, n = pend
                wait(dve, point["mm", n])
                if n > 0:
                    wait(dve, point["add", n - 1])
                b = dve.value_load(base[0:1, g:g + 1], min_val=0, max_val=N - 1)
                win = acc[0:rows_a, ds(b, W)]
                point["add", n] = s_add.inc(dve.tensor_tensor(win, win, ps_g[n % NPS][0:rows_a, 0:W], ALU.add))

            for g in range(NG):
                n = turn[0]
                turn[0] += 1
                slot = n % NSLOT
                parts, nt = (P, NT) if g < G else (R, 1)
                if n >= NSLOT:
                    wait(pool, point["mm", n - NSLOT])
                    if k == 0:
                        wait(sp, point["mm", n - NSLOT])
                for t in range(nt):
                    idx = srcT[:, t, g:g + 1] if g < G else src_l[0:R, 0:1]
                    point["gat", n] = s_gat[slot].inc(pool.indirect_dma_start(
                        out=gbuf(slot)[0:parts, t, :], out_offset=None, in_=tables[k],
                        in_offset=bass.IndirectOffsetOnAxis(ap=idx, axis=0)), 16)
                if k == 0:
                    if g == 0:
                        wait(sp, p_t)
                    if g < G:
                        d = sp.dma_start(ebuf(slot), edge_g[g])
                    else:
                        d = sp.dma_start(ebuf(slot)[0:R, 0, :], edge_r)
                    point["edg", n] = s_edg[slot].inc(d, 16)
                if n >= NS:
                    wait(dve, point["mm", n - NS])
                if g < G:
                    rel = relT[:, :, g:g + 1].broadcast_to([P, NT, W])
                    it = iota[:, :].rearrange("p (a w) -> p a w", a=1).broadcast_to([P, NT, W])
                    ins = dve.tensor_tensor(sbuf(n % NS), rel, it, ALU.is_equal)
                else:
                    ins = dve.tensor_scalar(sbuf(n % NS)[0:R, 0, :], iota[0:R, :], rel_l[0:R, 2:3], None, ALU.is_equal)
                point["S", n] = s_S.inc(ins)
                wait(pe, point["S", n], point["gat", n])
                if k == 0:
                    wait(pe, point["edg", n])
                if n >= NPS:
                    wait(pe, point["add", n - NPS])
                for t in range(nt):
                    last = edge_matmuls(ps_g[n % NPS], t, parts, sbuf(n % NS), gbuf(slot),
                                        ebuf(slot) if k == 0 else None, t == 0, t == nt - 1)
                point["mm", n] = s_mm.inc(last)
                if pend is not None:
                    add(pend)
                pend = (g, n)
            add(pend)
            wait(dve, point["add", pend[1]])

        def take(eng, s, n=1):
            eng.wait_ge(s.h, n)
            eng.sem_clear(s.h)

        def slow_group(k, g, parts, nt):
            rows_a = F + 1 if k == 0 else F
            if parts == P:
                a, b = src_g[ds(g, 1)], dst_g[ds(g, 1)]
                a, b = (v.rearrange("a p t -> (a p) t") for v in (a, b))
                e = edge_g[ds(g, 1)].rearrange("a p t f -> (a p) t f")
            else:
                a, b = src_r, dst_r
                e = edge_r.rearrange("p (t f) -> p t f", t=1)
            sp.dma_start(g_src[0:parts, 0:nt], a).then_inc(t_src.h, 16)
            sp.dma_start(g_dst[0:parts, 0:nt], b).then_inc(t_dst.h, 16)
            if k == 0:
                sp.dma_start(ebuf(0)[0:parts, 0:nt, :], e).then_inc(t_edg.h, 16)
            take(pool, t_src, 16)
            for t in range(nt):
                pool.indirect_dma_start(
                    out=gbuf(0)[0:parts, t, :], out_offset=None, in_=tables[k],
                    in_offset=bass.IndirectOffsetOnAxis(ap=g_src[0:parts, t:t + 1], axis=0)).then_inc(t_gat.h, 16)
            take(dve, t_dst, 16)
            dve.tensor_copy(g_cur[0:parts, 0:nt], g_dst[0:parts, 0:nt]).then_inc(t_cur.h, 1)
            take(dve, t_cur)
            take(pe, t_gat, 16 * nt)
            if k == 0:
                take(pe, t_edg, 16)
            with nc.Fori(0, (N + W - 1) // W, 1, engines=[pe.engine, dve.engine]) as w:
                cur = g_cur[0:parts, 0:nt].rearrange("p (t a) -> p t a", a=1).broadcast_to([parts, nt, W])
                it = iota[0:parts, :].rearrange("p (a w) -> p a w", a=1).broadcast_to([parts, nt, W])
                dve.tensor_tensor(sbuf(0)[0:parts, 0:nt, :], cur, it, ALU.is_equal).then_inc(t_S.h, 1)
                take(pe, t_S)
                for t in range(nt):
                    last = edge_matmuls(ps_g[0], t, parts, sbuf(0), gbuf(0),
                                        ebuf(0) if k == 0 else None, t == 0, t == nt - 1)
                last.then_inc(t_mm.h, 1)
                take(dve, t_mm)
                dve.tensor_scalar(g_cur[0:parts, 0:nt], g_cur[0:parts, 0:nt], float(W), None,
                                  ALU.subtract).then_inc(t_cur.h, 1)
                win = acc[0:rows_a, ds(w * W, W)]
                dve.tensor_tensor(win, win, ps_g[0][0:rows_a, 0:W], ALU.add).then_inc(t_add.h, 1)
                take(dve, t_add)
                take(dve, t_cur)
            dve.sem_inc(t_end.h, 1)
            take(sp, t_end)

        def slow_pass(k, acc_ready):
            wait(pool, (s_tab.h, s_tab.n))
            wait(sp, p_t)
            wait(pe, p_ones)
            wait(dve, acc_ready)
            with nc.Fori(0, G, 1, engines=[e.engine for e in engines]) as g:
                slow_group(k, g, P, NT)
            slow_group(k, None, R, 1)

        def run_pass(k, acc_ready):
            with nc.If(fv):
                slow_pass(k, acc_ready)
            with nc.Else():
                fast_pass(k, acc_ready)
            p = s_pass.inc(dve.memset(sc[0:1, 7:8], 0.0))
            wait(dve, p)
            return p

        norm_table(0, p_x, None)
        p_acc = run_pass(0, p_zero)
        wait(sp, p_acc)
        p_d = s_deg.inc(sp.dma_start(deg_dram, acc[F:F + 1, 0:N]), 16)
        wait(sp, p_d)
        p_deg = s_deg.inc(sp.dma_start(dis[0:PN, :], deg_dram.rearrange("a (p j) -> (a p) j", p=PN)), 16)
        wait(dve, p_deg)
        p = V(dve.tensor_scalar(dis[0:PN, :], dis[0:PN, :], 1.0, None, ALU.add))
        wait(act, p)
        p = s_a.inc(act.activation(dis[0:PN, :], dis[0:PN, :], ACT.Sqrt))
        wait(dve, p)
        V(dve.reciprocal(dis[0:PN, :], dis[0:PN, :]))

        hidT = big
        CW = 500 if N % 500 == 0 else 250
        p_mh = {}
        p_hid = {}
        wait(pe, p_w, p_acc)
        wait(act, p_w)
        for c in range(N // CW):
            if c >= 2:
                wait(pe, p_hid[c - 2])
            p_mh[c] = s_p.inc(pe.matmul(ps_h[c % 2][:, 0:CW], w01[:, :], acc[0:F, c * CW:(c + 1) * CW],
                                        start=True, stop=True))
            wait(act, p_mh[c])
            p_hid[c] = s_a.inc(act.activation(hidT[:, c * CW:(c + 1) * CW], ps_h[c % 2][:, 0:CW], ACT.Relu,
                                              bias=b01c[:, 0:1]))
        wait(pe, p_hid[c])

        def by_node(featT, K, wt, use):
            freed = {}
            for c, j0 in enumerate(range(0, J, 8)):
                j1 = min(J, j0 + 8)
                ps = ps_t[c % 2]
                if c >= 2:
                    wait(pe, freed[c - 2])
                for j in range(j0, j1):
                    last = pe.matmul(ps[0:PN, (j - j0) * F:(j - j0 + 1) * F],
                                     featT[0:K, j:j + (PN - 1) * J + 1:J], wt[:, :], start=True, stop=True)
                p = s_p.inc(last)
                wait(dve, p)
                freed[c] = use(j0, j1, ps[0:PN, 0:(j1 - j0) * F].rearrange("p (j f) -> p j f", f=F))
            return p

        def bc_row(t, n):
            return t.rearrange("p (a f) -> p a f", a=1).broadcast_to([PN, n, F])

        wait(dve, p_w)
        by_node(hidT, HID, w02, lambda j0, j1, ps: V(dve.tensor_tensor(
            v3(C, j0, j1), ps, bc_row(rows[0:PN, 0, :], j1 - j0), ALU.add)))

        def node_sum(dst_ap, col):
            n = col.shape[1]
            wait(pe, (s_v.h, s_v.n))
            p = s_p.inc(pe.matmul(ps_s[0:PN, 0:n], ones[0:PN, 0:PN], col, start=True, stop=True))
            wait(dve, p)
            return p

        cf = C[0:PN, :].rearrange("p (j f) -> p f j", f=F)
        V(dve.tensor_reduce(st[0:PN, 0, :], cf, X, ALU.add))
        node_sum(None, st[0:PN, 0, :])
        V(dve.tensor_scalar(st[0:PN, 0, :], ps_s[0:PN, 0:F], 1.0 / N, None, ALU.mult))
        p = V(dve.tensor_tensor(v3(C, 0, J), v3(C, 0, J), bc_row(st[0:PN, 0, :], J), ALU.subtract))
        wait(act, p)
        p = s_a.inc(act.activation(H[0:PN, :], C[0:PN, :], ACT.Square))
        wait(dve, p)
        V(dve.tensor_reduce(st[0:PN, 1, :], H[0:PN, :].rearrange("p (j f) -> p f j", f=F), X, ALU.add))
        node_sum(None, st[0:PN, 1, :])
        p = V(dve.tensor_scalar(st[0:PN, 2, :], ps_s[0:PN, 0:F], 1.0 / N, None, ALU.mult))
        wait(act, p)
        p = s_a.inc(act.activation(st[0:PN, 2, :], st[0:PN, 2, :], ACT.Sqrt, bias=epst[0:PN, 0:1]))
        wait(dve, p)
        V(dve.reciprocal(st[0:PN, 2, :], st[0:PN, 2, :]))
        V(dve.tensor_tensor(st[0:PN, 2, :], st[0:PN, 2, :], rows[0:PN, 1, :], ALU.mult))
        p_x1 = []
        for c in range(NCH):
            j0, j1 = c * JC, (c + 1) * JC
            V(dve.tensor_tensor(v3(C, j0, j1), v3(C, j0, j1), bc_row(st[0:PN, 2, :], JC), ALU.mult))
            V(dve.tensor_tensor(v3(C, j0, j1), v3(C, j0, j1), bc_row(rows[0:PN, 2, :], JC), ALU.add))
            p_x1.append(V(dve.tensor_tensor(v3(X1, j0, j1), v3(X1, j0, j1), v3(C, j0, j1), ALU.add)))

        def self_loops(ready):
            freed = {}
            accv = acc[0:F, 0:N].rearrange("f (p j) -> f j p", j=J)
            for c, j0 in enumerate(range(0, J, 4)):
                j1 = min(J, j0 + 4)
                wait(pe, ready)
                if c >= 2:
                    wait(pe, freed[c - 2])
                for j in range(j0, j1):
                    last = pe.transpose(ps_h[c % 2][0:F, (j - j0) * PN:(j - j0 + 1) * PN],
                                        H[0:PN, j * F:(j + 1) * F], ident[0:PN, 0:PN])
                p = s_p.inc(last)
                wait(act, p)
                freed[c] = s_a.inc(act.copy(accv[:, j0:j1, :], ps_h[c % 2][0:F, 0:(j1 - j0) * PN]
                                            .rearrange("f (j p) -> f j p", p=PN)))
            return freed[c]

        V(dve.tensor_scalar(w12a[:, :], w12[:, :], GW, None, ALU.mult))
        p_w12 = V(dve.scalar_tensor_tensor(out=w12b[:, :], in0=w12[:, :], scalar=1.0 - GW, in1=w12a[:, :],
                                           op0=ALU.mult, op1=ALU.add))
        wait(pe, p_w12)

        done = norm_table(1, p_x1, dis)
        p_acc = run_pass(1, self_loops(done[-1]))
        wait(pe, p_acc)

        def conv(bias, last_op):
            def use(j0, j1, ps):
                V(dve.tensor_tensor(v3(C, j0, j1), ps, bc_f(dis, j0, j1), ALU.mult))
                V(dve.tensor_tensor(v3(C, j0, j1), v3(C, j0, j1), bc_row(rows[0:PN, bias, :], j1 - j0), ALU.add))
                return last_op(j0, j1)
            return use

        by_node(acc, F, w11, conv(3, lambda j0, j1: V(dve.scalar_tensor_tensor(
            out=v3(H, j0, j1), in0=v3(C, j0, j1), scalar=0.0, in1=bc_f(dis, j0, j1),
            op0=ALU.max, op1=ALU.mult))))
        p_h = (s_v.h, s_v.n)
        wait(sp, p_h)
        s_tab.inc(sp.dma_start(tables[2].rearrange("(p j) f -> p (j f)", p=PN), H[0:PN, :]), 16)
        p_acc = run_pass(2, self_loops(p_h))
        wait(pe, p_acc)
        by_node(acc, F, w12b, conv(4, lambda j0, j1: V(dve.tensor_scalar(
            C[0:PN, j0 * F:j1 * F], C[0:PN, j0 * F:j1 * F], 0.0, None, ALU.max))))

        V(dve.tensor_reduce(sc[0:PN, 0:1], C[0:PN, :], X, ALU.add))
        node_sum(None, sc[0:PN, 0:1])
        V(dve.tensor_scalar(sc[0:PN, 1:2], ps_s[0:PN, 0:1], 1.0 / (N * F), None, ALU.mult))
        p = V(dve.tensor_scalar(C[0:PN, :], C[0:PN, :], sc[0:PN, 1:2], None, ALU.subtract))
        wait(act, p)
        p = s_a.inc(act.activation(H[0:PN, :], C[0:PN, :], ACT.Square, accum_out=sc[0:PN, 2:3]))
        wait(pe, p)
        node_sum(None, sc[0:PN, 2:3])
        p = V(dve.tensor_scalar(sc[0:PN, 3:4], ps_s[0:PN, 0:1], 1.0 / (N * F), None, ALU.mult))
        wait(act, p)
        p = s_a.inc(act.activation(sc[0:PN, 3:4], sc[0:PN, 3:4], ACT.Sqrt, bias=epst[0:PN, 0:1]))
        wait(dve, p)
        V(dve.reciprocal(sc[0:PN, 3:4], sc[0:PN, 3:4]))
        V(dve.tensor_tensor(sc[0:PN, 3:4], sc[0:PN, 3:4], lnwb[0:PN, 0:1], ALU.mult))
        outv = out.rearrange("(p j) f -> p (j f)", p=PN)
        for c in range(NCH):
            a, b = c * JC * F, (c + 1) * JC * F
            V(dve.tensor_scalar(C[0:PN, a:b], C[0:PN, a:b], sc[0:PN, 3:4], lnwb[0:PN, 1:2], ALU.mult, ALU.add))
            p = V(dve.tensor_tensor(X1[0:PN, a:b], X1[0:PN, a:b], C[0:PN, a:b], ALU.add))
            wait(sp, p)
            s_out.inc(sp.dma_start(outv[:, a:b], X1[0:PN, a:b]), 16)
        sp.wait_ge(s_out.h, s_out.n)
        sp.wait_ge(s_tab.h, s_tab.n)
        sp.wait_ge(s_deg.h, s_deg.n)


_INS = ['x', 'src', 'dst', 'edge_attr_64', 'L0_gnn_W1', 'L0_gnn_b1', 'L0_gnn_W2', 'L0_gnn_b2',
        'L0_gnn_bn_gamma', 'L0_gnn_bn_beta', 'L1_gnn_W1', 'L1_gnn_b1', 'L1_gnn_W2', 'L1_gnn_b2',
        'L1_gnn_ln_w', 'L1_gnn_ln_b']


def kernel(**inputs):
    import numpy as _np
    import concourse.bacc as _bacc
    from concourse import mybir as _mybir
    from concourse.bass_utils import run_bass_kernel_spmd as _run

    nc = _bacc.Bacc("TRN2", target_bir_lowering=False, num_devices=1)
    arrays, args = {}, []
    for name in _INS:
        a = _np.ascontiguousarray(inputs[name])
        arrays[f"in_{name}_dram"] = a
        args.append(nc.dram_tensor(f"in_{name}_dram", a.shape, _mybir.dt.from_np(a.dtype), kind="ExternalInput").ap())
    out = nc.dram_tensor("out_0_dram", inputs['x'].shape, _mybir.dt.float32, kind="ExternalOutput").ap()
    bass_gnn_preln_kernel(nc, *args, out)
    r = _run(nc, [arrays], core_ids=[0])
    return r.results[0]["out_0_dram"]
```

```python
from contextlib import ExitStack

import concourse.bass as bass
from concourse import mybir

ALU = mybir.AluOpType
ACT = mybir.ActivationFunctionType
F32 = mybir.dt.float32
I32 = mybir.dt.int32
F16 = mybir.dt.float16
BF16 = mybir.dt.bfloat16
X = mybir.AxisListType.X
ds = bass.ds

P = 128
F = 64
HID = 128
PN = 125
W = 128
NT = 10
VR = 12
NSLOT = 4
NEDGE = 4
NS = 2
NOH = 3
LAG = 11
DENSE = (46, 62, 62)
EPS = 1e-05
MAGIC = 12582912.0
GW = 0.8


class Sem:

    def __init__(self, handle):
        self.h = handle
        self.n = 0

    def inc(self, ins, by=1):
        ins.then_inc(self.h, by)
        self.n += by
        return (self.h, self.n)


def bass_gnn_preln_kernel(nc, x, src, dst, edge, W01, b01, W02, b02, gamma, beta,
                          W11, b11, W12, b12, ln_w, ln_b, out):
    N = x.shape[0]
    E = src.shape[0]
    J = N // PN
    G = E // (P * NT)
    R = (E - G * P * NT) // 2
    assert N == J * PN and 1 < R <= P and E == G * P * NT + 2 * R
    NG = G + 1
    JF = J * F
    dense = [min(d, G) for d in DENSE]
    DM = max(dense)
    DG = min(dense)
    DT = DM * NT
    VJ = VR * J
    KC = 4 * J
    assert KC <= 512 and VR == 12 and NT * VR <= P and VJ <= 2048

    pe, act, dve, pool, sp = nc.tensor, nc.scalar, nc.vector, nc.gpsimd, nc.sync

    def wait(eng, *points):
        for h, n in points:
            eng.wait_ge(h, n)

    with ExitStack() as ctx:
        def sb(name, shape, dt=F32):
            return ctx.enter_context(nc.sbuf_tensor(name, shape, dt))

        def sem(name):
            return Sem(ctx.enter_context(nc.semaphore(name)))

        def dram(name, shape):
            return nc.dram_tensor(name, shape, F32, kind="Internal").ap()

        tables = [dram(f"table{k}", [N, F]) for k in range(3)]
        deg_dram = dram("deg_dram", [1, N])
        x1_dram = dram("x1_dram", [N, F])

        o_A = [3 * J * F // 2, 3 * J * F // 2 + P * J // 2]
        o_oh = o_A[1] + P * J // 2
        o_ob = o_oh + NOH * VJ // 2
        o_g = o_ob + NT * PN
        o_e = o_g + NSLOT * NT * F
        o_S = o_e + NEDGE * NT * (F + 1)
        o_v = o_S + NS * NT * W
        AR = o_v + 2 * (F + W)

        acc = sb("acc", [P, N + W])
        arena = sb("arena", [P, AR])
        X1 = arena[:, 0:JF]
        H = arena[:, o_A[0]:o_A[0] + JF]
        C = arena[:, o_A[1]:o_A[1] + JF]
        hidT = arena[:, 0:N]
        assert N <= o_A[1] and JF == P * J // 2
        srcT = sb("srcT", [P, NT, G - DG], I32)
        relT = sb("relT", [P, NT, G])
        keyT = sb("keyT", [P, DT])
        hibT = sb("hibT", [P, DT])
        rowT = sb("rowT", [P, DM])
        iota16 = sb("iota16", [P, VJ], F16)
        mt = sb("mt", [P, 4])
        src_l = sb("src_l", [P, 2], I32)
        dst_l = sb("dst_l", [P, 2], I32)
        dstb_l = sb("dstb_l", [P, 1], I32)
        rel_l = sb("rel_l", [P, 5])
        base = sb("base", [1, NG], I32)
        iota_i = sb("iota_i", [P, W], I32)
        iota = sb("iota", [P, W])
        rowid = sb("rowid", [P, 1], I32)
        rowf = sb("rowf", [P, 1])
        ident = sb("ident", [P, P])
        ones = sb("ones", [P, P])
        w01 = sb("w01", [F, HID])
        w02 = sb("w02", [HID, F])
        w11 = sb("w11", [F, F])
        w12 = sb("w12", [F, F])
        w12a = sb("w12a", [F, F])
        w12b = sb("w12b", [F, F])
        b01c = sb("b01c", [HID, 1])
        rows = sb("rows", [P, 5, F])
        lnwb = sb("lnwb", [P, 2])
        mean = sb("mean", [P, J])
        var = sb("var", [P, J])
        dis = sb("dis", [P, J])
        st = sb("st", [P, 4, F])
        sc = sb("sc", [P, 8])
        epst = sb("epst", [P, 1])
        mm = sb("mm", [P, 16])
        flag = sb("flag", [1, 1], I32)
        g_src = sb("g_src", [P, NT], I32)
        g_dst = sb("g_dst", [P, NT], I32)
        g_cur = sb("g_cur", [P, NT])

        psum = ctx.enter_context(nc.psum_tensor("psum", [P, 8, 512], F32))
        ps_b = [psum[:, 3 * i:3 * i + 3, :] for i in range(2)]
        ps_v = psum[:, 6, 0:3 * F]
        ps_g = psum[:, 7, 0:W]
        ps_t = [psum[:, i, :] for i in range(2)]
        ps_h = [psum[:, 3 + i, :] for i in range(2)]
        ps_s = psum[:, 6, :]

        Xs = arena[:, 0:o_A[0]].bitcast(BF16).rearrange("p (j s f) -> p j s f", s=3, f=F)
        A = [arena[:, o:o + P * J // 2].bitcast(BF16) for o in o_A]

        def part(o, k, n):
            return arena[:, o + k * n:o + (k + 1) * n]

        def oh(k):
            return part(o_oh, k, VJ // 2).bitcast(F16)

        def ob(k):
            return part(o_ob, k, NT * PN // 2).bitcast(F16).rearrange("p (t b) -> p t b", b=PN)

        def gbuf(k):
            return part(o_g, k, NT * F).rearrange("p (t f) -> p t f", f=F)

        def ebuf(k):
            return part(o_e, k, NT * (F + 1)).rearrange("p (t f) -> p t f", f=F + 1)

        def sbuf(k):
            return part(o_S, k, NT * W).rearrange("p (t w) -> p t w", w=W)

        def vbuf(k):
            return part(o_v, k, F + W)

        s_c = sem("s_c")
        s_in = [sem(f"s_in{i}") for i in range(6)]
        s_v = sem("s_v")
        s_a = sem("s_a")
        s_p = sem("s_p")
        s_k = sem("s_k")
        s_tab = sem("s_tab")
        s_deg = sem("s_deg")
        s_out = sem("s_out")
        s_gat = [sem(f"s_gat{i}") for i in range(NSLOT)]
        s_edg = [sem(f"s_edg{i}") for i in range(NEDGE)]
        s_oh = sem("s_oh")
        s_bld = sem("s_bld")
        s_ev = sem("s_ev")
        s_app = sem("s_app")
        s_fld = sem("s_fld")
        s_x1 = sem("s_x1")
        s_S = sem("s_S")
        s_mm = sem("s_mm")
        s_add = sem("s_add")
        s_pass = sem("s_pass")
        t_src = sem("t_src")
        t_dst = sem("t_dst")
        t_edg = sem("t_edg")
        t_gat = sem("t_gat")
        t_gd = sem("t_gd")
        t_cur = sem("t_cur")
        t_S = sem("t_S")
        t_mm = sem("t_mm")
        t_add = sem("t_add")
        t_end = sem("t_end")

        def V(ins):
            p = s_v.inc(ins)
            wait(dve, p)
            return p

        edge_g = edge[0:G * P * NT, :].rearrange("(g p t) f -> g p t f", p=P, t=NT)
        edge_r = edge[G * P * NT:E, :].rearrange("(p t) f -> p t f", t=2)
        src_g = src[0:G * P * NT].rearrange("(g p t) -> g p t", p=P, t=NT)
        dst_g = dst[0:G * P * NT].rearrange("(g p t) -> g p t", p=P, t=NT)
        src_r = src[G * P * NT:E].rearrange("(p t) -> p t", t=2)
        dst_r = dst[G * P * NT:E].rearrange("(p t) -> p t", t=2)
        blocks = [(b, min(P, G - b)) for b in range(0, G, P)]
        NB = len(blocks)
        EG = P * NT

        def raw(k, b, r):
            return acc[0:r, (k * NB + b) * EG:(k * NB + b + 1) * EG]

        tblocks = [(b, min(P, DT - b)) for b in range(0, DT, P)]
        TB = len(tblocks)
        o_raw = 2 * NB * EG

        def raw_t(k, b, r):
            o = o_raw + (k * TB + b) * P
            return acc[0:r, o:o + P]

        assert o_raw + 2 * TB * P <= N + W and o_oh + 2 * NB * EG + 5 * TB * P + P <= AR

        xv = x.rearrange("(p j) f -> p (j f)", p=PN)
        for k, a in ((0, dst), (1, src)):
            for b, (g0, r) in enumerate(blocks):
                rows_d = a[g0 * EG:(g0 + r) * EG].rearrange("(g e) -> g e", e=EG)
                p_raw = s_in[k].inc(sp.dma_start(raw(k, b, r).bitcast(I32), rows_d), 16)
            for b, (t0, r) in enumerate(tblocks):
                rows_d = a[t0 * P:(t0 + r) * P].rearrange("(g e) -> g e", e=P)
                p_raw = s_in[k].inc(sp.dma_start(raw_t(k, b, r).bitcast(I32), rows_d), 16)
            if k == 0:
                p_dst = p_raw
            else:
                p_src = p_raw
        NCH = 4
        JC = J // NCH if J % NCH == 0 else J
        NCH = J // JC
        p_x = []
        for c in range(NCH):
            s = s_in[2] if c == 0 else sem(f"s_xc{c}")
            p_x.append(s.inc(act.dma_start(X1[0:PN, c * JC * F:(c + 1) * JC * F],
                                           xv[:, c * JC * F:(c + 1) * JC * F]), 16))
        s_in[3].inc(sp.dma_start(base[0:1, 0:G], dst[0:G * EG].rearrange("(g e) -> e g", e=EG)[0:1, :],
                                allow_slow_non_contiguous=True), 16)
        s_in[3].inc(sp.dma_start(base[0:1, G:NG], dst[G * EG:G * EG + 1].rearrange("(a b) -> a b", a=1)), 16)
        s_in[3].inc(sp.dma_start(src_l[0:R, :], src_r), 16)
        s_in[3].inc(sp.dma_start(dst_l[0:R, :], dst_r), 16)
        p_small = s_in[3].inc(sp.dma_start(
            dstb_l[0:R, :], dst[G * EG:G * EG + 1].rearrange("(a b) -> a b", a=1).broadcast_to([R, 1])), 16)
        for t, a in ((w01, W01), (w02, W02), (w11, W11), (w12, W12)):
            s_in[4].inc(sp.dma_start(t[:, :], a), 16)
        s_in[4].inc(sp.dma_start(b01c[:, :], b01.rearrange("(a b) -> a b", b=1)), 16)
        for i, a in enumerate((b02, gamma, beta, b11, b12)):
            s_in[4].inc(sp.dma_start(rows[:, i, :], a.rearrange("(a b) -> a b", a=1).broadcast_to([P, F])), 16)
        for i, a in enumerate((ln_w, ln_b)):
            p_w = s_in[4].inc(sp.dma_start(lnwb[:, i:i + 1], a.rearrange("(a b) -> a b", a=1).broadcast_to([P, 1])), 16)

        p_i0 = s_k.inc(pool.iota(iota_i[:, :], pattern=[[1, W]], base=0, channel_multiplier=0))
        p_i1 = s_k.inc(pool.iota(rowid[:, :], pattern=[[0, 1]], base=0, channel_multiplier=1))
        iota_w = C[:, 0:VJ].bitcast(I32)
        p_i1 = s_k.inc(pool.iota(iota_w[:, :], pattern=[[1, VJ]], base=0, channel_multiplier=0))
        wait(dve, p_i1)
        p_i16 = V(dve.tensor_copy(iota16[:, :], iota_w))
        V(dve.tensor_copy(iota[:, :], iota_i[:, :]))
        V(dve.tensor_copy(rowf[:, :], rowid[:, :]))
        p_id = V(dve.tensor_scalar(ident[:, :], iota[:, 0:P], rowf[:, 0:1], None, ALU.is_equal))
        V(dve.memset(epst[:, :], EPS))
        V(dve.memset(mm[:, :], 0.0))
        p_ones = V(dve.memset(ones[:, :], 1.0))

        relf = [part(o_oh, b, EG)[0:r] for b, (g0, r) in enumerate(blocks)]
        srcf = [part(o_oh, NB + b, EG)[0:r] for b, (g0, r) in enumerate(blocks)]
        o_t = o_oh + 2 * NB * EG

        def tile_f(k):
            return part(o_t, k, TB * P)

        rowf_g = part(o_t + 5 * TB * P, 0, P)
        wait(dve, p_dst)
        for b, (g0, r) in enumerate(blocks):
            V(dve.tensor_copy(relf[b], raw(0, b, r).bitcast(I32)))
            V(dve.tensor_copy(mm[0:r, 15:16], relf[b][:, 0:1]))
            V(dve.tensor_scalar(relf[b], relf[b], mm[0:r, 15:16], None, ALU.subtract))
            V(dve.tensor_reduce(mm[0:r, 4 * b:4 * b + 1], relf[b], X, ALU.max))
            V(dve.tensor_reduce(mm[0:r, 4 * b + 1:4 * b + 2], relf[b], X, ALU.min))
        wait(dve, p_src)
        for b, (g0, r) in enumerate(blocks):
            p_raw2 = V(dve.tensor_copy(srcf[b], raw(1, b, r).bitcast(I32)))
        tdst, tsrc, tkey, tb, tq_ = (tile_f(i) for i in range(5))
        V(dve.memset(mt[:, :], 0.0))
        for b, (t0, r) in enumerate(tblocks):
            c0, c1 = b * P, (b + 1) * P
            V(dve.tensor_copy(tdst[0:r, c0:c1], raw_t(0, b, r).bitcast(I32)))
            V(dve.tensor_copy(tsrc[0:r, c0:c1], raw_t(1, b, r).bitcast(I32)))
            V(dve.tensor_copy(mt[0:r, 0:1], tdst[0:r, c0:c0 + 1]))
            V(dve.tensor_scalar(tdst[0:r, c0:c1], tdst[0:r, c0:c1], mt[0:r, 0:1], None, ALU.subtract))
            V(dve.tensor_reduce(mt[0:r, 1:2], tdst[0:r, c0:c1], X, ALU.max))
            V(dve.tensor_reduce(mt[0:r, 2:3], tdst[0:r, c0:c1], X, ALU.min))
            V(dve.tensor_scalar(mt[0:r, 1:2], mt[0:r, 1:2], float(W - VR), None, ALU.add))
            V(dve.tensor_tensor(mm[0:r, 4:5], mm[0:r, 4:5], mt[0:r, 1:2], ALU.max))
            V(dve.tensor_tensor(mm[0:r, 5:6], mm[0:r, 5:6], mt[0:r, 2:3], ALU.min))
            a, q = tsrc[0:r, c0:c1], tq_[0:r, c0:c1]
            V(dve.tensor_scalar(q, a, 1.0 / J, 0.5 / J - 0.5, ALU.mult, ALU.add))
            V(dve.tensor_scalar(q, q, MAGIC, None, ALU.add))
            V(dve.tensor_scalar(tb[0:r, c0:c1], q, MAGIC, None, ALU.subtract))
            V(dve.scalar_tensor_tensor(out=q, in0=tb[0:r, c0:c1], scalar=-float(J), in1=a,
                                       op0=ALU.mult, op1=ALU.add))
            p_tile = V(dve.scalar_tensor_tensor(out=tkey[0:r, c0:c1], in0=tdst[0:r, c0:c1], scalar=float(J),
                                                in1=q, op0=ALU.mult, op1=ALU.add))
        V(dve.memset(rowf_g, 0.0))
        NRB = [(g0, min(r, DM - g0)) for g0, r in blocks if g0 < DM]
        assert len(NRB) == 1
        rD = NRB[0][1]
        p_rows = V(dve.tensor_tensor(
            rowf_g[0:rD, 0:NT * VR].rearrange("p (t r) -> p t r", r=VR),
            relf[0][0:rD, 0:EG:P].rearrange("p (t a) -> p t a", a=1).broadcast_to([rD, NT, VR]),
            iota[0:rD, 0:VR].rearrange("p (a r) -> p a r", a=1).broadcast_to([rD, NT, VR]), ALU.add))
        wait(dve, p_small)
        V(dve.tensor_copy(rel_l[0:R, 0:2], dst_l[0:R, :]))
        V(dve.tensor_copy(rel_l[0:R, 4:5], dstb_l[0:R, :]))
        V(dve.tensor_scalar(rel_l[0:R, 2:4], rel_l[0:R, 0:2], rel_l[0:R, 4:5], None, ALU.subtract))
        V(dve.tensor_copy(mm[0:R, 12:14], rel_l[0:R, 2:4]))
        V(dve.tensor_reduce(mm[:, 14:15], mm[:, 0:14], X, ALU.max))
        V(dve.tensor_reduce(mm[:, 15:16], mm[:, 0:14], X, ALU.min))
        V(dve.tensor_scalar(mm[:, 0:1], mm[:, 14:15], float(W - 1), None, ALU.is_gt))
        V(dve.tensor_scalar(mm[:, 1:2], mm[:, 15:16], 0.0, None, ALU.is_lt))
        p_f = V(dve.tensor_tensor(mm[:, 2:3], mm[:, 0:1], mm[:, 1:2], ALU.add))

        tq = []
        k = 0
        free = {}
        nt_b = 512 // G if G < 512 else 1
        nt_b = min(nt_b, NT)
        for what, mats in (("src", srcf), ("rel", relf)):
            for t0 in range(0, NT, nt_b):
                n = min(nt_b, NT - t0)
                pt = ps_t[k % 2]
                wait(pe, p_raw2, p_id, *([free[k - 2]] if k >= 2 else []))
                for i in range(n):
                    for b, (g0, r) in enumerate(blocks):
                        last = pe.transpose(pt[:, i * G + g0:i * G + g0 + r],
                                            mats[b][:, t0 + i:EG:NT], ident[0:r, 0:r])
                p_t = s_p.inc(last)
                wait(dve, p_t)
                pv = pt[:, 0:n * G].rearrange("p (t g) -> p t g", g=G)
                if what == "src":
                    ins = dve.tensor_copy(srcT[:, t0:t0 + n, :], pv[:, :, DG:G])
                else:
                    ins = dve.tensor_copy(relT[:, t0:t0 + n, :], pv)
                free[k] = V(ins)
                k += 1
            if what == "src":
                p_srcT = free[k - 1]
        for what, mat, tgt in (("key", tkey, keyT), ("hib", tb, hibT)):
            for b0 in range(0, TB, 4):
                bs = tblocks[b0:b0 + 4]
                pt = ps_t[k % 2]
                wait(pe, p_tile, free[k - 2])
                for b, (t0, r) in enumerate(bs):
                    last = pe.transpose(pt[:, b * P:b * P + r], mat[0:r, (b0 + b) * P:(b0 + b + 1) * P],
                                        ident[0:r, 0:r])
                p_t = s_p.inc(last)
                wait(dve, p_t)
                n = bs[-1][0] + bs[-1][1] - bs[0][0]
                free[k] = V(dve.tensor_copy(tgt[:, b0 * P:b0 * P + n], pt[:, 0:n]))
                k += 1
        wait(pe, p_rows, free[k - 2])
        p_t = s_p.inc(pe.transpose(ps_t[k % 2][:, 0:rD], rowf_g[0:rD, :], ident[0:rD, 0:rD]))
        wait(dve, p_t)
        free[k] = V(dve.tensor_copy(rowT[:, 0:rD], ps_t[k % 2][:, 0:rD]))
        k += 1
        p_relT = free[k - 1]
        wait(pe, p_f, p_ones)
        p_fs = s_p.inc(pe.matmul(ps_s[0:1, 0:1], mm[:, 2:3], ones[:, 0:1], start=True, stop=True))
        wait(dve, p_fs)
        V(dve.tensor_scalar(mm[0:1, 3:4], ps_s[0:1, 0:1], 0.0, None, ALU.is_gt))
        p_flag = V(dve.tensor_copy(flag[:, :], mm[0:1, 3:4]))
        wait(dve, p_t)
        p_zero = V(dve.memset(acc[:, :], 0.0))

        engines = [pe, act, dve, pool, sp]
        for eng in engines:
            wait(eng, p_flag)
        fv = nc.values_load(flag[0:1, 0:1], engines=[e.engine for e in engines], min_val=0, max_val=1)

        def bc_f(t, j0, j1):
            return t[0:PN, j0:j1].rearrange("p (j a) -> p j a", a=1).broadcast_to([PN, j1 - j0, F])

        def v3(t, j0, j1):
            return t[0:PN, j0 * F:j1 * F].rearrange("p (j f) -> p j f", f=F)

        def norm_table(k, ready, scale):
            done = []
            for c in range(NCH):
                j0, j1 = c * JC, (c + 1) * JC
                wait(dve, ready[c])
                V(dve.tensor_reduce(mean[0:PN, j0:j1], v3(X1, j0, j1), X, ALU.add))
                V(dve.tensor_scalar(mean[0:PN, j0:j1], mean[0:PN, j0:j1], 1.0 / F, None, ALU.mult))
                p = V(dve.tensor_tensor(v3(H, j0, j1), v3(X1, j0, j1), bc_f(mean, j0, j1), ALU.subtract))
                wait(act, p)
                p = s_a.inc(act.activation(C[0:PN, j0 * F:j1 * F], H[0:PN, j0 * F:j1 * F], ACT.Square))
                wait(dve, p)
                p = V(dve.tensor_reduce(var[0:PN, j0:j1], v3(C, j0, j1), X, ALU.add))
                wait(act, p)
                p = s_a.inc(act.activation(var[0:PN, j0:j1], var[0:PN, j0:j1], ACT.Sqrt,
                                           bias=epst[0:PN, 0:1], scale=1.0 / F))
                wait(dve, p)
                V(dve.reciprocal(var[0:PN, j0:j1], var[0:PN, j0:j1]))
                if scale is not None:
                    V(dve.tensor_tensor(var[0:PN, j0:j1], var[0:PN, j0:j1], scale[0:PN, j0:j1], ALU.mult))
                p = V(dve.scalar_tensor_tensor(out=v3(H, j0, j1), in0=v3(H, j0, j1), scalar=0.0,
                                               in1=bc_f(var, j0, j1), op0=ALU.max, op1=ALU.mult))
                wait(sp, p)
                done.append(p)
                s_tab.inc(sp.dma_start(tables[k].rearrange("(p j) f -> p (j f)", p=PN)[:, j0 * F:j1 * F],
                                       H[0:PN, j0 * F:j1 * F]), 16)
            return done

        def split_table(ready):
            for c in range(NCH):
                j0, j1 = c * JC, (c + 1) * JC
                p = ready[c]
                src_t = H
                for i in range(3):
                    wait(act, p)
                    p = s_a.inc(act.copy(Xs[0:PN, j0:j1, i, :], v3(src_t, j0, j1)))
                    wait(dve, p)
                    if i < 2:
                        p = V(dve.tensor_tensor(v3(C, j0, j1), v3(src_t, j0, j1), Xs[0:PN, j0:j1, i, :],
                                                ALU.subtract))
                    src_t = C
            return p

        turn = {"S": 0, "g": 0, "w": 0}
        point = {}

        def jobs_of(nt, gb, eb):
            jobs = [(eb, 0, F + 1)] if eb is not None else []
            jobs += [(gb, t, F) for t in range(nt)] if gb is not None else []
            jobs += [(eb, t, F + 1) for t in range(1, nt)] if eb is not None else []
            return jobs

        def run_jobs(ps, jobs, S, parts, row=None):
            n = len(jobs) + (row is not None)
            order = list(jobs)
            if row is not None:
                order.insert(min(1, len(jobs)), None)
            for i, job in enumerate(order):
                a, z = i == 0, i == n - 1
                if job is None:
                    last = pe.matmul(ps[0:F, :], row[:, 0:F], row[:, F:F + W], start=a, stop=z)
                else:
                    buf, t, m = job
                    last = pe.matmul(ps[0:m, :], buf[0:parts, t, 0:m], S[0:parts, t, :], start=a, stop=z)
            return last

        def fast_pass(k):
            rows_a = F + 1 if k == 0 else F
            D = dense[k]
            steps = D * NT
            gl = list(range(D, NG))
            events = []
            for s in range(steps + LAG + 4):
                events.append((s + 0.5, 1, "step", s))
            for i in range(D):
                events.append((i * NT + NT - 1 + LAG + 3.6, 2, "win", i))
            span = (steps + LAG + 4) if D else 1
            for q, g in enumerate(gl):
                events.append(((q + 1.2) * span / (len(gl) + 0.4), 3, "gat", g))
            events.sort()
            uses = [(kind, g) for _, _, kind, g in events if kind != "step"]
            s_uses = [u for u in uses if u[0] == "gat" or k == 0]
            seq_s = {u: turn["S"] + n for n, u in enumerate(s_uses)}
            seq_e = {u: n for n, u in enumerate(uses)}
            seq_g = {u: turn["g"] + n for n, u in enumerate(g2 for g2 in uses if g2[0] == "gat")}
            seq_w = {u: turn["w"] + n for n, u in enumerate(uses)}
            order_s = list(s_uses)
            order_g = [u for u in uses if u[0] == "gat"]
            made = {"S": 0, "g": 0, "e": 0}

            def shape(u):
                return (P, NT) if u[1] < G else (R, 2)

            def make_S(upto):
                while made["S"] < min(upto, len(order_s)):
                    u = order_s[made["S"]]
                    made["S"] += 1
                    n, g = seq_s[u], u[1]
                    if ("Sfree", n - NS) in point:
                        wait(dve, point["Sfree", n - NS])
                    if g < G:
                        rel = relT[:, :, g:g + 1].broadcast_to([P, NT, W])
                        it = iota[:, :].rearrange("p (a w) -> p a w", a=1).broadcast_to([P, NT, W])
                        ins = dve.tensor_tensor(sbuf(n % NS), rel, it, ALU.is_equal)
                    else:
                        rel = rel_l[0:R, 2:4].rearrange("p (t a) -> p t a", a=1).broadcast_to([R, 2, W])
                        it = iota[0:R, :].rearrange("p (a w) -> p a w", a=1).broadcast_to([R, 2, W])
                        ins = dve.tensor_tensor(sbuf(n % NS)[0:R, 0:2, :], rel, it, ALU.is_equal)
                    point["S", n] = s_S.inc(ins)

            def gather(upto):
                while made["g"] < min(upto, len(order_g)):
                    u = order_g[made["g"]]
                    made["g"] += 1
                    n, g = seq_g[u], u[1]
                    parts, nt = shape(u)
                    if ("gfree", n - NSLOT) in point:
                        wait(pool, point["gfree", n - NSLOT])
                    for t in range(nt):
                        idx = srcT[:, t, g - DG:g - DG + 1] if g < G else src_l[0:R, t:t + 1]
                        point["gat", n] = s_gat[n % NSLOT].inc(pool.indirect_dma_start(
                            out=gbuf(n % NSLOT)[0:parts, t, :], out_offset=None, in_=tables[k],
                            in_offset=bass.IndirectOffsetOnAxis(ap=idx, axis=0)), 16)

            def load_edges(upto):
                while k == 0 and made["e"] < min(upto, len(uses)):
                    n = made["e"]
                    g = uses[n][1]
                    made["e"] += 1
                    if n >= NEDGE:
                        wait(sp, point["efree", n - NEDGE])
                    if g < G:
                        d = sp.dma_start(ebuf(n % NEDGE)[:, :, 0:F], edge_g[g])
                    else:
                        d = sp.dma_start(ebuf(n % NEDGE)[0:R, 0:2, 0:F], edge_r)
                    point["edg", n] = s_edg[n % NEDGE].inc(d, 16)

            pend = None

            def add(w, g):
                wait(dve, point["mm", w])
                if ("add", w - 1) in point:
                    wait(dve, point["add", w - 1])
                b = dve.value_load(base[0:1, g:g + 1], min_val=0, max_val=N - 1)
                win = acc[0:rows_a, ds(b, W)]
                point["add", w] = s_add.inc(dve.tensor_tensor(win, win, ps_g[0:rows_a, :], ALU.add))

            def make_ob(i):
                if i < D:
                    if ("bld", k, i * NT - NT - 1) in point:
                        wait(dve, point["bld", k, i * NT - NT - 1])
                    src_v = hibT[:, i * NT:(i + 1) * NT].rearrange("p (t a) -> p t a", a=1)
                    it = iota16[:, 0:PN].rearrange("p (a b) -> p a b", a=1).broadcast_to([P, NT, PN])
                    point["ob", i] = s_oh.inc(dve.tensor_tensor(ob(i % 2), src_v.broadcast_to([P, NT, PN]), it,
                                                                ALU.is_equal))

            def make_oh(s):
                if s < steps:
                    if s >= NOH:
                        wait(dve, point["bld", k, s - NOH])
                    point["oh", s] = s_oh.inc(dve.tensor_scalar(oh(s % NOH), iota16[:, :], keyT[:, s:s + 1], None,
                                                                ALU.is_equal))

            def step(s):
                nonlocal pend
                i, t = s // NT, s % NT
                if pend is not None:
                    add(*pend)
                    pend = None
                if t == 4:
                    make_ob(i + 1)
                make_oh(s + NOH - 1)
                if s < steps:
                    wait(pe, point["oh", s])
                    if t == 0:
                        wait(pe, point["ob", i])
                    if s >= 2:
                        wait(pe, point["ev", s - 2])
                    for c in range(3):
                        last = pe.matmul(ps_b[s % 2][0:PN, c, 0:KC], ob(i % 2)[:, t, :],
                                         oh(s % NOH)[:, c * KC:(c + 1) * KC], start=True, stop=True)
                    point["bld", k, s] = s_bld.inc(last)
                a = s - LAG
                if 0 <= a < steps:
                    ai, at = a // NT, a % NT
                    if at == 0:
                        wait(pe, point["ev", ai * NT + NT - 1])
                        if ai >= 1:
                            wait(pe, point["fold", ai - 1])
                    for j in range(at * J // NT, (at + 1) * J // NT):
                        last = pe.matmul(ps_v, A[ai % 2][0:PN, j:(P - 1) * J + j + 1:J],
                                         Xs[0:PN, j, :, :], start=(j == 0), stop=(j == J - 1))
                    if at == NT - 1:
                        point["app", ai] = s_app.inc(last)
                if s < steps:
                    wait(act, point["bld", k, s])
                    if t == 0 and i >= 2:
                        wait(act, point["app", i - 2])
                    point["ev", s] = s_ev.inc(act.copy(
                        A[i % 2][0:PN, t * VJ:(t + 1) * VJ].rearrange("p (c k) -> p c k", c=3),
                        ps_b[s % 2][0:PN, :, 0:KC]))
                f = s - LAG
                if f >= 0 and f % NT == NT - 1 and f < steps:
                    fi = f // NT
                    wait(dve, point["app", fi])
                    if fi >= 2:
                        wait(dve, point["win", fi - 2])
                    v = vbuf(fi % 2)
                    dve.tensor_scalar(v[:, F:F + W], iota[:, :], rowT[:, fi:fi + 1], None, ALU.is_equal)
                    point["fold", fi] = s_fld.inc(dve.tensor_reduce(
                        v[:, 0:F], ps_v.rearrange("p (s f) -> p f s", s=3), X, ALU.add))

            def use(u):
                nonlocal pend
                kind, g = u
                parts, nt = shape(u)
                n_e, w = seq_e[u], seq_w[u]
                if pend is not None:
                    add(*pend)
                if u in seq_s:
                    wait(pe, point["S", seq_s[u]])
                S = sbuf(seq_s[u] % NS) if u in seq_s else None
                gb = row = eb = None
                if kind == "gat":
                    wait(pe, point["gat", seq_g[u]])
                    gb = gbuf(seq_g[u] % NSLOT)
                else:
                    wait(pe, point["fold", g])
                    row = vbuf(g % 2)
                if k == 0:
                    wait(pe, point["edg", n_e])
                    eb = ebuf(n_e % NEDGE)
                if w > 0:
                    wait(pe, point["add", w - 1])
                last = run_jobs(ps_g, jobs_of(nt, gb, eb), S, parts, row)
                p = s_mm.inc(last)
                point["mm", w] = p
                if kind == "gat":
                    point["gfree", seq_g[u]] = p
                else:
                    point["win", g] = p
                if u in seq_s:
                    point["Sfree", seq_s[u]] = p
                    make_S(order_s.index(u) + 1 + NS)
                if kind == "gat":
                    gather(order_g.index(u) + 1 + NSLOT)
                if k == 0:
                    point["efree", n_e] = p
                    load_edges(n_e + 1 + NEDGE)
                pend = (w, g)

            gather(NSLOT)
            load_edges(NEDGE)
            make_ob(0)
            for s in range(NOH - 1):
                make_oh(s)
            make_S(NS)
            for _, _, kind, v in events:
                if kind == "step":
                    step(v)
                else:
                    use((kind, v))
            if pend is not None:
                add(*pend)
            wait(dve, point["add", turn["w"] + len(uses) - 1])
            turn["S"] += len(s_uses)
            turn["g"] += len(order_g)
            turn["w"] += len(uses)

        def take(eng, s, n=1):
            eng.wait_ge(s.h, n)
            eng.sem_clear(s.h)

        def slow_group(k, g, parts, nt):
            rows_a = F + 1 if k == 0 else F
            if parts == P:
                a, b = src_g[ds(g, 1)], dst_g[ds(g, 1)]
                a, b = (v.rearrange("a p t -> (a p) t") for v in (a, b))
                e = edge_g[ds(g, 1)].rearrange("a p t f -> (a p) t f")
            else:
                a, b = src_r, dst_r
                e = edge_r
            sp.dma_start(g_src[0:parts, 0:nt], a).then_inc(t_src.h, 16)
            sp.dma_start(g_dst[0:parts, 0:nt], b).then_inc(t_dst.h, 16)
            if k == 0:
                sp.dma_start(ebuf(0)[0:parts, 0:nt, 0:F], e).then_inc(t_edg.h, 16)
            take(pool, t_src, 16)
            for t in range(nt):
                pool.indirect_dma_start(
                    out=gbuf(0)[0:parts, t, :], out_offset=None, in_=tables[k],
                    in_offset=bass.IndirectOffsetOnAxis(ap=g_src[0:parts, t:t + 1], axis=0)).then_inc(t_gat.h, 16)
            pool.wait_ge(t_gat.h, 16 * nt)
            pool.dma_reset(range(t_gat.h.num, t_gat.h.num + 1))
            pool.sem_clear(t_gat.h)
            pool.sem_inc(t_gd.h, 1)
            take(dve, t_dst, 16)
            dve.tensor_copy(g_cur[0:parts, 0:nt], g_dst[0:parts, 0:nt]).then_inc(t_cur.h, 1)
            take(dve, t_cur)
            take(pe, t_gd)
            if k == 0:
                take(pe, t_edg, 16)
            with nc.Fori(0, (N + W - 1) // W, 1, engines=[pe.engine, dve.engine]) as w:
                cur = g_cur[0:parts, 0:nt].rearrange("p (t a) -> p t a", a=1).broadcast_to([parts, nt, W])
                it = iota[0:parts, :].rearrange("p (a w) -> p a w", a=1).broadcast_to([parts, nt, W])
                dve.tensor_tensor(sbuf(0)[0:parts, 0:nt, :], cur, it, ALU.is_equal).then_inc(t_S.h, 1)
                take(pe, t_S)
                last = run_jobs(ps_g, jobs_of(nt, gbuf(0), ebuf(0) if k == 0 else None),
                                sbuf(0), parts)
                last.then_inc(t_mm.h, 1)
                take(dve, t_mm)
                dve.tensor_scalar(g_cur[0:parts, 0:nt], g_cur[0:parts, 0:nt], float(W), None,
                                  ALU.subtract).then_inc(t_cur.h, 1)
                win = acc[0:rows_a, ds(w * W, W)]
                dve.tensor_tensor(win, win, ps_g[0:rows_a, 0:W], ALU.add).then_inc(t_add.h, 1)
                take(dve, t_add)
                take(dve, t_cur)
            dve.sem_inc(t_end.h, 1)
            take(sp, t_end)

        def slow_pass(k):
            with nc.Fori(0, G, 1, engines=[e.engine for e in engines]) as g:
                slow_group(k, g, P, NT)
            slow_group(k, None, R, 2)

        def run_pass(k, acc_ready, ready):
            tab = (s_tab.h, s_tab.n)
            wait(pool, p_srcT, p_small, p_t, tab)
            wait(sp, p_t)
            for q in range(2):
                V(dve.memset(vbuf(q), 0.0))
            if k == 0:
                for q in range(NEDGE):
                    p = V(dve.memset(ebuf(q)[:, :, F:F + 1], 1.0))
            if k == 1:
                wait(act, (s_x1.h, s_x1.n))
            p_xs = split_table(ready)
            wait(dve, acc_ready, tab)
            for q in range(2):
                p = V(dve.memset(A[q][0:PN, NT * VJ:P * J], 0.0))
            wait(pe, p_xs, p)
            wait(act, p)
            with nc.If(fv):
                slow_pass(k)
            with nc.Else():
                fast_pass(k)
            p = s_pass.inc(dve.memset(sc[0:1, 7:8], 0.0))
            wait(dve, p)
            return p

        done = norm_table(0, p_x, None)
        p_acc = run_pass(0, p_zero, done)
        wait(sp, p_acc)
        p_d = s_deg.inc(sp.dma_start(deg_dram, acc[F:F + 1, 0:N]), 16)
        wait(sp, p_d)
        p_deg = s_deg.inc(sp.dma_start(dis[0:PN, :], deg_dram.rearrange("a (p j) -> (a p) j", p=PN)), 16)
        wait(dve, p_deg)
        p = V(dve.tensor_scalar(dis[0:PN, :], dis[0:PN, :], 1.0, None, ALU.add))
        wait(act, p)
        p = s_a.inc(act.activation(dis[0:PN, :], dis[0:PN, :], ACT.Sqrt))
        wait(dve, p)
        V(dve.reciprocal(dis[0:PN, :], dis[0:PN, :]))

        CW = 500 if N % 500 == 0 else 250
        p_mh = {}
        p_hid = {}
        wait(pe, p_w, p_acc)
        wait(act, p_w)
        for c in range(N // CW):
            if c >= 2:
                wait(pe, p_hid[c - 2])
            p_mh[c] = s_p.inc(pe.matmul(ps_h[c % 2][:, 0:CW], w01[:, :], acc[0:F, c * CW:(c + 1) * CW],
                                        start=True, stop=True))
            wait(act, p_mh[c])
            p_hid[c] = s_a.inc(act.activation(hidT[:, c * CW:(c + 1) * CW], ps_h[c % 2][:, 0:CW], ACT.Relu,
                                              bias=b01c[:, 0:1]))
        wait(pe, p_hid[c])

        def by_node(featT, K, wt, use):
            freed = {}
            for c, j0 in enumerate(range(0, J, 8)):
                j1 = min(J, j0 + 8)
                ps = ps_t[c % 2]
                if c >= 2:
                    wait(pe, freed[c - 2])
                for j in range(j0, j1):
                    last = pe.matmul(ps[0:PN, (j - j0) * F:(j - j0 + 1) * F],
                                     featT[0:K, j:j + (PN - 1) * J + 1:J], wt[:, :], start=True, stop=True)
                p = s_p.inc(last)
                wait(dve, p)
                freed[c] = use(j0, j1, ps[0:PN, 0:(j1 - j0) * F].rearrange("p (j f) -> p j f", f=F))
            return p

        def bc_row(t, n):
            return t.rearrange("p (a f) -> p a f", a=1).broadcast_to([PN, n, F])

        wait(dve, p_w)
        p = by_node(hidT, HID, w02, lambda j0, j1, ps: V(dve.tensor_tensor(
            v3(C, j0, j1), ps, bc_row(rows[0:PN, 0, :], j1 - j0), ALU.add)))

        wait(sp, p)
        p_xr = s_x1.inc(sp.dma_start(X1[0:PN, :], xv), 16)

        def node_sum(dst_ap, col):
            n = col.shape[1]
            wait(pe, (s_v.h, s_v.n))
            p = s_p.inc(pe.matmul(ps_s[0:PN, 0:n], ones[0:PN, 0:PN], col, start=True, stop=True))
            wait(dve, p)
            return p

        cf = C[0:PN, :].rearrange("p (j f) -> p f j", f=F)
        V(dve.tensor_reduce(st[0:PN, 0, :], cf, X, ALU.add))
        node_sum(None, st[0:PN, 0, :])
        V(dve.tensor_scalar(st[0:PN, 0, :], ps_s[0:PN, 0:F], 1.0 / N, None, ALU.mult))
        p = V(dve.tensor_tensor(v3(C, 0, J), v3(C, 0, J), bc_row(st[0:PN, 0, :], J), ALU.subtract))
        wait(act, p)
        p = s_a.inc(act.activation(H[0:PN, :], C[0:PN, :], ACT.Square))
        wait(dve, p)
        V(dve.tensor_reduce(st[0:PN, 1, :], H[0:PN, :].rearrange("p (j f) -> p f j", f=F), X, ALU.add))
        node_sum(None, st[0:PN, 1, :])
        p = V(dve.tensor_scalar(st[0:PN, 2, :], ps_s[0:PN, 0:F], 1.0 / N, None, ALU.mult))
        wait(act, p)
        p = s_a.inc(act.activation(st[0:PN, 2, :], st[0:PN, 2, :], ACT.Sqrt, bias=epst[0:PN, 0:1]))
        wait(dve, p)
        V(dve.reciprocal(st[0:PN, 2, :], st[0:PN, 2, :]))
        V(dve.tensor_tensor(st[0:PN, 2, :], st[0:PN, 2, :], rows[0:PN, 1, :], ALU.mult))
        p_x1 = []
        for c in range(NCH):
            j0, j1 = c * JC, (c + 1) * JC
            V(dve.tensor_tensor(v3(C, j0, j1), v3(C, j0, j1), bc_row(st[0:PN, 2, :], JC), ALU.mult))
            V(dve.tensor_tensor(v3(C, j0, j1), v3(C, j0, j1), bc_row(rows[0:PN, 2, :], JC), ALU.add))
            wait(dve, p_xr)
            p_x1.append(V(dve.tensor_tensor(v3(X1, j0, j1), v3(X1, j0, j1), v3(C, j0, j1), ALU.add)))
            wait(sp, p_x1[-1])
            s_x1.inc(sp.dma_start(x1_dram.rearrange("(p j) f -> p (j f)", p=PN)[:, j0 * F:j1 * F],
                                  X1[0:PN, j0 * F:j1 * F]), 16)

        def self_loops(ready):
            freed = {}
            accv = acc[0:F, 0:N].rearrange("f (p j) -> f j p", j=J)
            for c, j0 in enumerate(range(0, J, 4)):
                j1 = min(J, j0 + 4)
                wait(pe, ready)
                if c >= 2:
                    wait(pe, freed[c - 2])
                for j in range(j0, j1):
                    last = pe.transpose(ps_h[c % 2][0:F, (j - j0) * PN:(j - j0 + 1) * PN],
                                        H[0:PN, j * F:(j + 1) * F], ident[0:PN, 0:PN])
                p = s_p.inc(last)
                wait(act, p)
                freed[c] = s_a.inc(act.copy(accv[:, j0:j1, :], ps_h[c % 2][0:F, 0:(j1 - j0) * PN]
                                            .rearrange("f (j p) -> f j p", p=PN)))
            return freed[c]

        V(dve.tensor_scalar(w12a[:, :], w12[:, :], GW, None, ALU.mult))
        p_w12 = V(dve.scalar_tensor_tensor(out=w12b[:, :], in0=w12[:, :], scalar=1.0 - GW, in1=w12a[:, :],
                                           op0=ALU.mult, op1=ALU.add))
        wait(pe, p_w12)

        done = norm_table(1, p_x1, dis)
        p_acc = run_pass(1, self_loops(done[-1]), done)
        wait(pe, p_acc)

        def conv(bias, last_op):
            def use(j0, j1, ps):
                V(dve.tensor_tensor(v3(C, j0, j1), ps, bc_f(dis, j0, j1), ALU.mult))
                V(dve.tensor_tensor(v3(C, j0, j1), v3(C, j0, j1), bc_row(rows[0:PN, bias, :], j1 - j0), ALU.add))
                return last_op(j0, j1)
            return use

        by_node(acc, F, w11, conv(3, lambda j0, j1: V(dve.scalar_tensor_tensor(
            out=v3(H, j0, j1), in0=v3(C, j0, j1), scalar=0.0, in1=bc_f(dis, j0, j1),
            op0=ALU.max, op1=ALU.mult))))
        p_h = (s_v.h, s_v.n)
        wait(sp, p_h)
        s_tab.inc(sp.dma_start(tables[2].rearrange("(p j) f -> p (j f)", p=PN), H[0:PN, :]), 16)
        p_acc = run_pass(2, self_loops(p_h), [p_h] * NCH)
        wait(sp, p_acc)
        p_xr = s_x1.inc(sp.dma_start(X1[0:PN, :], x1_dram.rearrange("(p j) f -> p (j f)", p=PN)), 16)
        wait(dve, p_xr)
        wait(pe, p_acc)
        by_node(acc, F, w12b, conv(4, lambda j0, j1: V(dve.tensor_scalar(
            C[0:PN, j0 * F:j1 * F], C[0:PN, j0 * F:j1 * F], 0.0, None, ALU.max))))

        V(dve.tensor_reduce(sc[0:PN, 0:1], C[0:PN, :], X, ALU.add))
        node_sum(None, sc[0:PN, 0:1])
        V(dve.tensor_scalar(sc[0:PN, 1:2], ps_s[0:PN, 0:1], 1.0 / (N * F), None, ALU.mult))
        p = V(dve.tensor_scalar(C[0:PN, :], C[0:PN, :], sc[0:PN, 1:2], None, ALU.subtract))
        wait(act, p)
        p = s_a.inc(act.activation(H[0:PN, :], C[0:PN, :], ACT.Square, accum_out=sc[0:PN, 2:3]))
        wait(pe, p)
        node_sum(None, sc[0:PN, 2:3])
        p = V(dve.tensor_scalar(sc[0:PN, 3:4], ps_s[0:PN, 0:1], 1.0 / (N * F), None, ALU.mult))
        wait(act, p)
        p = s_a.inc(act.activation(sc[0:PN, 3:4], sc[0:PN, 3:4], ACT.Sqrt, bias=epst[0:PN, 0:1]))
        wait(dve, p)
        V(dve.reciprocal(sc[0:PN, 3:4], sc[0:PN, 3:4]))
        V(dve.tensor_tensor(sc[0:PN, 3:4], sc[0:PN, 3:4], lnwb[0:PN, 0:1], ALU.mult))
        outv = out.rearrange("(p j) f -> p (j f)", p=PN)
        for c in range(NCH):
            a, b = c * JC * F, (c + 1) * JC * F
            V(dve.tensor_scalar(C[0:PN, a:b], C[0:PN, a:b], sc[0:PN, 3:4], lnwb[0:PN, 1:2], ALU.mult, ALU.add))
            p = V(dve.tensor_tensor(X1[0:PN, a:b], X1[0:PN, a:b], C[0:PN, a:b], ALU.add))
            wait(sp, p)
            s_out.inc(sp.dma_start(outv[:, a:b], X1[0:PN, a:b]), 16)
        sp.wait_ge(s_out.h, s_out.n)
        sp.wait_ge(s_tab.h, s_tab.n)
        sp.wait_ge(s_deg.h, s_deg.n)


_INS = ['x', 'src', 'dst', 'edge_attr_64', 'L0_gnn_W1', 'L0_gnn_b1', 'L0_gnn_W2', 'L0_gnn_b2',
        'L0_gnn_bn_gamma', 'L0_gnn_bn_beta', 'L1_gnn_W1', 'L1_gnn_b1', 'L1_gnn_W2', 'L1_gnn_b2',
        'L1_gnn_ln_w', 'L1_gnn_ln_b']


def kernel(**inputs):
    import numpy as _np
    import concourse.bacc as _bacc
    from concourse import mybir as _mybir
    from concourse.bass_utils import run_bass_kernel_spmd as _run

    nc = _bacc.Bacc("TRN2", target_bir_lowering=False, num_devices=1)
    arrays, args = {}, []
    for name in _INS:
        a = _np.ascontiguousarray(inputs[name])
        arrays[f"in_{name}_dram"] = a
        args.append(nc.dram_tensor(f"in_{name}_dram", a.shape, _mybir.dt.from_np(a.dtype), kind="ExternalInput").ap())
    out = nc.dram_tensor("out_0_dram", inputs['x'].shape, _mybir.dt.float32, kind="ExternalOutput").ap()
    bass_gnn_preln_kernel(nc, *args, out)
    r = _run(nc, [arrays], core_ids=[0])
    return r.results[0]["out_0_dram"]
```

```python
from contextlib import ExitStack

import concourse.bass as bass
from concourse import mybir

ALU = mybir.AluOpType
ACT = mybir.ActivationFunctionType
F32 = mybir.dt.float32
I32 = mybir.dt.int32
F16 = mybir.dt.float16
BF16 = mybir.dt.bfloat16
X = mybir.AxisListType.X
ds = bass.ds

P = 128
F = 64
HID = 128
PN = 125
W = 128
NT = 10
VR = 11
NSLOT = 4
NEDGE = 4
NS = 2
NOH = 3
LAG = 11
DENSE = (55, 67, 67)
EPS = 1e-05
MAGIC = 12582912.0
GW = 0.8


class Sem:

    def __init__(self, handle):
        self.h = handle
        self.n = 0

    def inc(self, ins, by=1):
        ins.then_inc(self.h, by)
        self.n += by
        return (self.h, self.n)


def bass_gnn_preln_kernel(nc, x, src, dst, edge, W01, b01, W02, b02, gamma, beta,
                          W11, b11, W12, b12, ln_w, ln_b, out):
    N = x.shape[0]
    E = src.shape[0]
    J = N // PN
    G = E // (P * NT)
    R = (E - G * P * NT) // 2
    assert N == J * PN and 1 < R <= P and E == G * P * NT + 2 * R
    NG = G + 1
    JF = J * F
    dense = [min(d, G) for d in DENSE]
    DM = max(dense)
    DG = min(dense)
    TB = (DM * NT + P - 1) // P
    VJ = VR * J
    KC = (VJ + 11) // 12 * 4
    VP = 3 * KC
    assert KC <= 512 and NT * VR <= P and VP <= 2048 and (NT - 1) * VJ + VP <= P * J

    pe, act, dve, pool, sp = nc.tensor, nc.scalar, nc.vector, nc.gpsimd, nc.sync

    def wait(eng, *points):
        for h, n in points:
            eng.wait_ge(h, n)

    with ExitStack() as ctx:
        def sb(name, shape, dt=F32):
            return ctx.enter_context(nc.sbuf_tensor(name, shape, dt))

        def sem(name):
            return Sem(ctx.enter_context(nc.semaphore(name)))

        def dram(name, shape):
            return nc.dram_tensor(name, shape, F32, kind="Internal").ap()

        table0 = dram("table0", [N, F])
        tables = [None] + [nc.dram_tensor(f"table{k}", [N, 3 * F], BF16, kind="Internal").ap() for k in (1, 2)]
        deg_dram = dram("deg_dram", [1, N])
        x1_dram = dram("x1_dram", [N, F])

        o_A = [3 * J * F // 2, 3 * J * F // 2 + P * J // 2]
        o_oh = o_A[1] + P * J // 2
        o_ob = o_oh + NOH * VP // 2
        o_g = o_ob + NT * PN
        o_e = o_g + NSLOT * NT * F
        o_S = o_e + NEDGE * NT * (F + 1)
        o_v = o_S + NS * NT * W
        o_q = o_v + 2 * (F + W)
        AR = o_q + F

        acc = sb("acc", [P, N + W])
        arena = sb("arena", [P, AR])
        X1 = arena[:, 0:JF]
        H = arena[:, o_A[0]:o_A[0] + JF]
        C = arena[:, o_A[1]:o_A[1] + JF]
        mean = arena[:, o_v:o_v + J]
        var = arena[:, o_v + J:o_v + 2 * J]
        pst = arena[:, o_e:o_e + (J + 7) // 8 * F].rearrange("p (c f) -> p c f", f=F)
        assert JF == P * J // 2 and 2 * J <= AR - o_v and NSLOT * NT * 3 * F // 2 <= o_S - o_g
        srcT = sb("srcT", [P, NT, G - DG], I32)
        relT = sb("relT", [P, NT, G])
        keyT = sb("keyT", [P, TB * P])
        hibT = sb("hibT", [P, TB * P])
        rowT = sb("rowT", [P, DM])
        iota16 = sb("iota16", [P, VP], F16)
        mt = sb("mt", [P, TB])
        src_l = sb("src_l", [P, 2], I32)
        dst_l = sb("dst_l", [P, 2], I32)
        dstb_l = sb("dstb_l", [P, 1], I32)
        rel_l = sb("rel_l", [P, 5])
        base = sb("base", [1, NG], I32)
        iota_i = sb("iota_i", [P, W], I32)
        iota = sb("iota", [P, W])
        rowid = sb("rowid", [P, 1], I32)
        rowf = sb("rowf", [P, 1])
        ident = sb("ident", [P, P])
        ones = sb("ones", [P, P])
        w01 = sb("w01", [F, HID])
        w02 = sb("w02", [HID, F])
        w11 = sb("w11", [F + 1, F])
        w12 = sb("w12", [F + 1, F])
        w12a = sb("w12a", [F, F])
        w12b = sb("w12b", [F + 1, F])
        b01c = sb("b01c", [HID, 1])
        rows = sb("rows", [P, 3, F])
        lnwb = sb("lnwb", [P, 2])
        dis = sb("dis", [P, J])
        dis2 = sb("dis2", [P, J])
        st = sb("st", [P, 4, F])
        sc = sb("sc", [P, 8])
        epst = sb("epst", [P, 1])
        mm = sb("mm", [P, 16])
        flag = sb("flag", [1, 1], I32)
        g_src = sb("g_src", [P, NT], I32)
        g_dst = sb("g_dst", [P, NT], I32)
        g_cur = sb("g_cur", [P, NT])

        psum = ctx.enter_context(nc.psum_tensor("psum", [P, 8, 512], F32))
        ps_b = [psum[:, 3 * i:3 * i + 3, :] for i in range(2)]
        ps_v = psum[:, 6, 0:3 * F]
        ps_g = psum[:, 7, 0:W]
        ps_q = psum[:, 7, W:W + 3 * F]
        ps_t = [psum[:, i, :] for i in range(2)]
        ps_h = [psum[:, 3 + i, :] for i in range(2)]
        ps_s = psum[:, 6, :]

        Xs = arena[:, 0:o_A[0]].bitcast(BF16).rearrange("p (j s f) -> p j s f", s=3, f=F)
        A = [arena[:, o:o + P * J // 2].bitcast(BF16) for o in o_A]

        def part(o, k, n):
            return arena[:, o + k * n:o + (k + 1) * n]

        def oh(k):
            return part(o_oh, k, VP // 2).bitcast(F16)

        def ob(k):
            return part(o_ob, k, NT * PN // 2).bitcast(F16).rearrange("p (t b) -> p t b", b=PN)

        def gbuf(k):
            return part(o_g, k, NT * F).rearrange("p (t f) -> p t f", f=F)

        def ebuf(k):
            return part(o_e, k, NT * (F + 1)).rearrange("p (t f) -> p t f", f=F + 1)

        def sbuf(k):
            return part(o_S, k, NT * W).rearrange("p (t w) -> p t w", w=W)

        def gbuf_s(k):
            return part(o_g, k, NT * 3 * F // 2).bitcast(BF16).rearrange("p (t f) -> p t f", f=3 * F)

        def sbuf_s(k):
            return part(o_S, k, NT * W // 2).bitcast(BF16).rearrange("p (t w) -> p t w", w=W)

        qbuf = arena[:, o_q:o_q + F]

        def vbuf(k):
            return part(o_v, k, F + W)

        s_c = sem("s_c")
        s_in = [sem(f"s_in{i}") for i in range(6)]
        s_v = sem("s_v")
        s_a = sem("s_a")
        s_p = sem("s_p")
        s_k = sem("s_k")
        s_tab = sem("s_tab")
        s_deg = sem("s_deg")
        s_out = sem("s_out")
        s_gat = [sem(f"s_gat{i}") for i in range(NSLOT)]
        s_edg = [sem(f"s_edg{i}") for i in range(NEDGE)]
        s_oh = sem("s_oh")
        s_bld = sem("s_bld")
        s_ev = sem("s_ev")
        s_app = sem("s_app")
        s_fld = sem("s_fld")
        s_pre = sem("s_pre")
        s_sq = sem("s_sq")
        s_x1 = sem("s_x1")
        s_S = sem("s_S")
        s_mm = sem("s_mm")
        s_add = sem("s_add")
        s_pass = sem("s_pass")
        t_src = sem("t_src")
        t_dst = sem("t_dst")
        t_edg = sem("t_edg")
        t_gat = sem("t_gat")
        t_gd = sem("t_gd")
        t_cur = sem("t_cur")
        t_S = sem("t_S")
        t_mm = sem("t_mm")
        t_add = sem("t_add")
        t_end = sem("t_end")

        def V(ins):
            p = s_v.inc(ins)
            wait(dve, p)
            return p

        edge_g = edge[0:G * P * NT, :].rearrange("(g p t) f -> g p t f", p=P, t=NT)
        edge_r = edge[G * P * NT:E, :].rearrange("(p t) f -> p t f", t=2)
        src_g = src[0:G * P * NT].rearrange("(g p t) -> g p t", p=P, t=NT)
        dst_g = dst[0:G * P * NT].rearrange("(g p t) -> g p t", p=P, t=NT)
        src_r = src[G * P * NT:E].rearrange("(p t) -> p t", t=2)
        dst_r = dst[G * P * NT:E].rearrange("(p t) -> p t", t=2)
        blocks = [(b, min(P, G - b)) for b in range(0, G, P)]
        NB = len(blocks)
        EG = P * NT

        def raw(k, b, r):
            return acc[0:r, (k * NB + b) * EG:(k * NB + b + 1) * EG]

        tblocks = [(b * P, P) for b in range(TB)]
        assert TB * P <= G * NT
        o_raw = 2 * NB * EG

        def raw_t(k, b, r, n=1):
            o = o_raw + (k * TB + b) * P
            return acc[0:r, o:o + n * P]

        assert o_raw + 2 * TB * P <= N + W

        xv = x.rearrange("(p j) f -> p (j f)", p=PN)
        for k, a in ((1, src), (0, dst)):
            for b, (g0, r) in enumerate(blocks):
                rows_d = a[g0 * EG:(g0 + r) * EG].rearrange("(g e) -> g e", e=EG)
                p_raw = s_in[k].inc(sp.dma_start(raw(k, b, r).bitcast(I32), rows_d), 16)
            for b, (t0, r) in enumerate(tblocks):
                rows_d = a[t0 * P:(t0 + r) * P].rearrange("(g e) -> g e", e=P)
                p_raw = s_in[k].inc(sp.dma_start(raw_t(k, b, r).bitcast(I32), rows_d), 16)
            if k == 0:
                p_dst = p_raw
            else:
                p_src = p_raw
        NCH = 4
        JC = J // NCH if J % NCH == 0 else J
        NCH = J // JC
        p_x = []
        for c in range(NCH):
            s = s_in[2] if c == 0 else sem(f"s_xc{c}")
            p_x.append(s.inc(act.dma_start(X1[0:PN, c * JC * F:(c + 1) * JC * F],
                                           xv[:, c * JC * F:(c + 1) * JC * F]), 16))
        s_in[3].inc(sp.dma_start(base[0:1, 0:G], dst[0:G * EG].rearrange("(g e) -> e g", e=EG)[0:1, :],
                                allow_slow_non_contiguous=True), 16)
        s_in[3].inc(sp.dma_start(base[0:1, G:NG], dst[G * EG:G * EG + 1].rearrange("(a b) -> a b", a=1)), 16)
        s_in[3].inc(sp.dma_start(src_l[0:R, :], src_r), 16)
        s_in[3].inc(sp.dma_start(dst_l[0:R, :], dst_r), 16)
        p_small = s_in[3].inc(sp.dma_start(
            dstb_l[0:R, :], dst[G * EG:G * EG + 1].rearrange("(a b) -> a b", a=1).broadcast_to([R, 1])), 16)
        for t, a in ((w01[:, :], W01), (w02[:, :], W02), (w11[0:F, :], W11), (w12[0:F, :], W12),
                     (w11[F:F + 1, :], b11.rearrange("(a b) -> a b", a=1)),
                     (w12b[F:F + 1, :], b12.rearrange("(a b) -> a b", a=1))):
            s_in[4].inc(sp.dma_start(t, a), 16)
        s_in[4].inc(sp.dma_start(b01c[:, :], b01.rearrange("(a b) -> a b", b=1)), 16)
        for i, a in enumerate((b02, gamma, beta)):
            s_in[4].inc(sp.dma_start(rows[:, i, :], a.rearrange("(a b) -> a b", a=1).broadcast_to([P, F])), 16)
        for i, a in enumerate((ln_w, ln_b)):
            p_w = s_in[4].inc(sp.dma_start(lnwb[:, i:i + 1], a.rearrange("(a b) -> a b", a=1).broadcast_to([P, 1])), 16)

        p_i0 = s_k.inc(pool.iota(iota_i[:, :], pattern=[[1, W]], base=0, channel_multiplier=0))
        p_i1 = s_k.inc(pool.iota(rowid[:, :], pattern=[[0, 1]], base=0, channel_multiplier=1))
        iota_w = C[:, 0:VP].bitcast(I32)
        p_i1 = s_k.inc(pool.iota(iota_w[:, :], pattern=[[1, VP]], base=0, channel_multiplier=0))
        wait(dve, p_i1)
        p_i16 = V(dve.tensor_copy(iota16[:, :], iota_w))
        V(dve.tensor_copy(iota[:, :], iota_i[:, :]))
        V(dve.tensor_copy(rowf[:, :], rowid[:, :]))
        p_id = V(dve.tensor_scalar(ident[:, :], iota[:, 0:P], rowf[:, 0:1], None, ALU.is_equal))
        V(dve.memset(epst[:, :], EPS))
        V(dve.memset(mm[:, :], 0.0))
        p_ones = V(dve.memset(ones[:, :], 1.0))

        relf = [part(o_oh, b, EG)[0:r] for b, (g0, r) in enumerate(blocks)]
        srcf = [part(o_g, b, EG)[0:r] for b, (g0, r) in enumerate(blocks)]
        o_t = max(o_e, o_g + NB * EG)
        assert o_oh + NB * EG <= o_g and o_t + 5 * TB * P + P <= o_v

        def tile_f(k):
            return part(o_t, k, TB * P)

        rowf_g = part(o_t + 5 * TB * P, 0, P)
        tdst, tsrc, tkey, tb, tq = (tile_f(i) for i in range(5))
        assert 4 * NB <= 10
        wait(act, p_src)
        for b, (g0, r) in enumerate(blocks):
            p_raw2 = s_a.inc(act.copy(srcf[b], raw(1, b, r).bitcast(I32)))
        s_a.inc(act.copy(tsrc, raw_t(1, 0, P, TB).bitcast(I32)))
        wait(act, p_dst)
        for b, (g0, r) in enumerate(blocks):
            s_a.inc(act.copy(relf[b], raw(0, b, r).bitcast(I32)))
        p_dstf = s_a.inc(act.copy(tdst, raw_t(0, 0, P, TB).bitcast(I32)))

        def prepare_dst():
            wait(dve, p_dstf)
            for b, (g0, r) in enumerate(blocks):
                V(dve.tensor_copy(mm[0:r, 15:16], relf[b][:, 0:1]))
                V(dve.tensor_scalar(relf[b], relf[b], mm[0:r, 15:16], None, ALU.subtract))
                V(dve.tensor_reduce(mm[0:r, 4 * b:4 * b + 1], relf[b], X, ALU.max))
                V(dve.tensor_reduce(mm[0:r, 4 * b + 1:4 * b + 2], relf[b], X, ALU.min))
            first = mt[:, :].rearrange("p (b a) -> p b a", a=1)
            V(dve.tensor_copy(mt[:, :], tdst[:, 0:TB * P:P]))
            V(dve.tensor_tensor(tdst.rearrange("p (b e) -> p b e", e=P), tdst.rearrange("p (b e) -> p b e", e=P),
                                first.broadcast_to([P, TB, P]), ALU.subtract))
            V(dve.tensor_reduce(mm[:, 10:11], tdst, X, ALU.max))
            V(dve.tensor_scalar(mm[:, 10:11], mm[:, 10:11], float(W - VR), None, ALU.add))
            V(dve.tensor_reduce(mm[:, 11:12], tdst, X, ALU.min))
            V(dve.tensor_scalar(tq, tsrc, 1.0 / J, 0.5 / J - 0.5, ALU.mult, ALU.add))
            V(dve.tensor_scalar(tq, tq, MAGIC, None, ALU.add))
            V(dve.tensor_scalar(tb, tq, MAGIC, None, ALU.subtract))
            V(dve.scalar_tensor_tensor(out=tq, in0=tb, scalar=-float(J), in1=tsrc, op0=ALU.mult, op1=ALU.add))
            return V(dve.scalar_tensor_tensor(out=tkey, in0=tdst, scalar=float(J), in1=tq,
                                              op0=ALU.mult, op1=ALU.add))

        turn_t = {"k": 0}
        freed_t = {}
        nt_b = min(NT, 512 // G if G < 512 else 1)

        def turned(write, take, *ready):
            k = turn_t["k"]
            turn_t["k"] += 1
            pt = ps_t[k % 2]
            wait(pe, *ready, p_id, *([freed_t[k - 2]] if k >= 2 else []))
            p = s_p.inc(write(pt))
            wait(dve, p)
            freed_t[k] = V(take(pt))
            return freed_t[k]

        def turn_edges(mats, take, *ready):
            for t0 in range(0, NT, nt_b):
                n = min(nt_b, NT - t0)

                def write(pt):
                    for i in range(n):
                        for b, (g0, r) in enumerate(blocks):
                            last = pe.transpose(pt[:, i * G + g0:i * G + g0 + r],
                                                mats[b][:, t0 + i:EG:NT], ident[0:r, 0:r])
                    return last

                p = turned(write, lambda pt: take(t0, n, pt[:, 0:n * G].rearrange("p (t g) -> p t g", g=G)), *ready)
            return p

        p_srcT = turn_edges(srcf, lambda t0, n, pv: dve.tensor_copy(srcT[:, t0:t0 + n, :], pv[:, :, DG:G]), p_raw2)

        def bc_f(t, j0, j1):
            return t[0:PN, j0:j1].rearrange("p (j a) -> p j a", a=1).broadcast_to([PN, j1 - j0, F])

        def v3(t, j0, j1):
            return t[0:PN, j0 * F:j1 * F].rearrange("p (j f) -> p j f", f=F)

        def norm_table(k, ready, scale):
            done, part_b = [], []
            for c in range(NCH):
                j0, j1 = c * JC, (c + 1) * JC
                wait(dve, ready[c])
                V(dve.tensor_reduce(mean[0:PN, j0:j1], v3(X1, j0, j1), X, ALU.add))
                p = V(dve.tensor_scalar(mean[0:PN, j0:j1], mean[0:PN, j0:j1], 1.0 / F, None, ALU.mult))
                if c % 2:
                    p = V(dve.tensor_tensor(v3(H, j0, j1), v3(X1, j0, j1), bc_f(mean, j0, j1),
                                                      ALU.subtract))
                else:
                    wait(pool, p)
                    p = s_k.inc(pool.tensor_tensor(v3(H, j0, j1), v3(X1, j0, j1), bc_f(mean, j0, j1),
                                                   ALU.subtract))
                wait(act, p)
                part_b.append(s_a.inc(act.activation(C[0:PN, j0 * F:j1 * F], H[0:PN, j0 * F:j1 * F], ACT.Square)))
            for c in range(NCH):
                j0, j1 = c * JC, (c + 1) * JC
                wait(dve, part_b[c])
                p = V(dve.tensor_reduce(var[0:PN, j0:j1], v3(C, j0, j1), X, ALU.add))
                wait(act, p)
                part_b[c] = s_a.inc(act.activation(var[0:PN, j0:j1], var[0:PN, j0:j1], ACT.Sqrt,
                                                   bias=epst[0:PN, 0:1], scale=1.0 / F))
            for c in range(NCH):
                j0, j1 = c * JC, (c + 1) * JC
                wait(dve, part_b[c])
                V(dve.reciprocal(var[0:PN, j0:j1], var[0:PN, j0:j1]))
                if scale is not None:
                    V(dve.tensor_tensor(var[0:PN, j0:j1], var[0:PN, j0:j1], scale[0:PN, j0:j1], ALU.mult))
                p = V(dve.scalar_tensor_tensor(out=v3(H, j0, j1), in0=v3(H, j0, j1), scalar=0.0,
                                               in1=bc_f(var, j0, j1), op0=ALU.max, op1=ALU.mult))
                done.append(p)
                if k == 0:
                    wait(sp, p)
                    s_tab.inc(sp.dma_start(table0.rearrange("(p j) f -> p (j f)", p=PN)[:, j0 * F:j1 * F],
                                           H[0:PN, j0 * F:j1 * F]), 16)
            return done

        def split_part(k, p, c, i):
            j0, j1 = c * JC, (c + 1) * JC
            src_t = H if i == 0 else C
            wait(act, p[c])
            p[c] = s_a.inc(act.copy(Xs[0:PN, j0:j1, i, :], v3(src_t, j0, j1)))
            wait(dve, p[c])
            if i < 2:
                p[c] = V(dve.tensor_tensor(v3(C, j0, j1), v3(src_t, j0, j1), Xs[0:PN, j0:j1, i, :],
                                           ALU.subtract))
            elif k > 0:
                wait(sp, p[c])
                s_tab.inc(sp.dma_start(tables[k].rearrange("(p j) f -> p j f", p=PN)[:, j0:j1, :],
                                       arena[0:PN, 0:o_A[0]].bitcast(BF16).rearrange(
                                           "p (j f) -> p j f", f=3 * F)[:, j0:j1, :]), 16)

        def split_table(k, ready, did=()):
            p = list(ready)
            for i in range(3):
                for c in range(NCH):
                    if (c, i) not in did:
                        split_part(k, p, c, i)
            return p[-1]

        done = norm_table(0, p_x, None)
        wait(pool, p_dstf)
        p_zero = s_k.inc(pool.memset(acc[:, :], 0.0))
        p_tile = prepare_dst()
        V(dve.memset(rowf_g, 0.0))
        NRB = [(g0, min(r, DM - g0)) for g0, r in blocks if g0 < DM]
        assert len(NRB) == 1
        rD = NRB[0][1]
        p_rows = V(dve.tensor_tensor(
            rowf_g[0:rD, 0:NT * VR].rearrange("p (t r) -> p t r", r=VR),
            relf[0][0:rD, 0:EG:P].rearrange("p (t a) -> p t a", a=1).broadcast_to([rD, NT, VR]),
            iota[0:rD, 0:VR].rearrange("p (a r) -> p a r", a=1).broadcast_to([rD, NT, VR]), ALU.add))
        wait(dve, p_small)
        V(dve.tensor_copy(rel_l[0:R, 0:2], dst_l[0:R, :]))
        V(dve.tensor_copy(rel_l[0:R, 4:5], dstb_l[0:R, :]))
        V(dve.tensor_scalar(rel_l[0:R, 2:4], rel_l[0:R, 0:2], rel_l[0:R, 4:5], None, ALU.subtract))
        V(dve.tensor_copy(mm[0:R, 12:14], rel_l[0:R, 2:4]))
        V(dve.tensor_reduce(mm[:, 14:15], mm[:, 0:14], X, ALU.max))
        V(dve.tensor_reduce(mm[:, 15:16], mm[:, 0:14], X, ALU.min))
        V(dve.tensor_scalar(mm[:, 0:1], mm[:, 14:15], float(W - 1), None, ALU.is_gt))
        V(dve.tensor_scalar(mm[:, 1:2], mm[:, 15:16], 0.0, None, ALU.is_lt))
        p_f = V(dve.tensor_tensor(mm[:, 2:3], mm[:, 0:1], mm[:, 1:2], ALU.add))

        p_relT = turn_edges(relf, lambda t0, n, pv: dve.tensor_copy(relT[:, t0:t0 + n, :], pv), p_tile)
        for mat, tgt in ((tkey, keyT), (tb, hibT)):
            for b0 in range(0, TB, 4):
                n = min(4, TB - b0)

                def write(pt):
                    for b in range(n):
                        last = pe.transpose(pt[:, b * P:(b + 1) * P], mat[:, (b0 + b) * P:(b0 + b + 1) * P],
                                            ident[:, :])
                    return last

                turned(write, lambda pt: dve.tensor_copy(tgt[:, b0 * P:(b0 + n) * P], pt[:, 0:n * P]), p_tile)

        def write(pt):
            return pe.transpose(pt[:, 0:rD], rowf_g[0:rD, :], ident[0:rD, 0:rD])

        turned(write, lambda pt: dve.tensor_copy(rowT[:, 0:rD], pt[:, 0:rD]), p_rows)
        wait(pe, p_f, p_ones)
        p_fs = s_p.inc(pe.matmul(ps_s[0:1, 0:1], mm[:, 2:3], ones[:, 0:1], start=True, stop=True))
        wait(dve, p_fs)
        V(dve.tensor_scalar(mm[0:1, 3:4], ps_s[0:1, 0:1], 0.0, None, ALU.is_gt))
        p_flag = V(dve.tensor_copy(flag[:, :], mm[0:1, 3:4]))

        engines = [pe, act, dve, pool, sp]
        turn = {"S": 0, "g": 0, "w": 0}
        point = {}

        def jobs_of(nt, gb, eb):
            jobs = [(eb, t, F + 1) for t in range(nt)] if eb is not None else []
            if gb is not None:
                jobs[1:1] = [(gb, t, F) for t in range(nt)]
            return jobs

        def run_jobs(ps, jobs, S, parts, row=None):
            n = len(jobs) + (row is not None)
            order = list(jobs)
            if row is not None:
                order.insert(min(1, len(jobs)), None)
            for i, job in enumerate(order):
                a, z = i == 0, i == n - 1
                if job is None:
                    last = pe.matmul(ps[0:F, :], row[:, 0:F], row[:, F:F + W], start=a, stop=z)
                else:
                    buf, t, m = job
                    last = pe.matmul(ps[0:m, :], buf[0:parts, t, 0:m], S[0:parts, t, :], start=a, stop=z)
            return last

        def first_gathers():
            wait(pool, p_srcT, (s_tab.h, s_tab.n))
            for n in range(min(NSLOT, G - dense[0])):
                for t in range(NT):
                    point["gat", n] = s_gat[n].inc(pool.indirect_dma_start(
                        out=gbuf(n)[:, t, :], out_offset=None, in_=table0,
                        in_offset=bass.IndirectOffsetOnAxis(ap=srcT[:, t, dense[0] + n - DG:dense[0] + n - DG + 1],
                                                            axis=0)), 16)

        def fast_pass(k):
            rows_a = F + 1 if k == 0 else F
            D = dense[k]
            steps = D * NT
            gl = list(range(D, NG))
            events = []
            for s in range(steps + LAG + 4):
                events.append((s + 0.5, 1, "step", s))
            span = steps + LAG + 4
            wins = [(i * NT + NT - 1 + LAG + 2.6, i) for i in range(D)]
            n_uses = D + len(gl)
            q = 0
            while wins or gl:
                at = (q + 1) * span / (n_uses + 1)
                q += 1
                if wins and (wins[0][0] <= at or not gl):
                    ready_at, i = wins.pop(0)
                    events.append((max(at, ready_at), 2, "win", i))
                else:
                    events.append((at, 3, "gat", gl.pop(0)))
            events.sort()
            uses = [(kind, g) for _, _, kind, g in events if kind != "step"]
            s_uses = [u for u in uses if u[0] == "gat" or k == 0]
            seq_s = {u: turn["S"] + n for n, u in enumerate(s_uses)}
            seq_e = {u: n for n, u in enumerate(uses)}
            seq_g = {u: turn["g"] + n for n, u in enumerate(g2 for g2 in uses if g2[0] == "gat")}
            seq_w = {u: turn["w"] + n for n, u in enumerate(uses)}
            order_s = list(s_uses)
            order_g = [u for u in uses if u[0] == "gat"]
            made = {"S": 0, "g": min(NSLOT, G - D) if k == 0 else 0, "e": 0}

            def shape(u):
                return (P, NT) if u[1] < G else (R, 2)

            def S_of(n):
                return sbuf(n % NS) if k == 0 else sbuf_s(n % NS)

            def g_of(n):
                return gbuf(n % NSLOT) if k == 0 else gbuf_s(n % NSLOT)

            def make_S(upto):
                while made["S"] < min(upto, len(order_s)):
                    u = order_s[made["S"]]
                    made["S"] += 1
                    n, g = seq_s[u], u[1]
                    if ("Sfree", n - NS) in point:
                        wait(dve, point["Sfree", n - NS])
                    if g < G:
                        rel = relT[:, :, g:g + 1].broadcast_to([P, NT, W])
                        it = iota[:, :].rearrange("p (a w) -> p a w", a=1).broadcast_to([P, NT, W])
                        ins = dve.tensor_tensor(S_of(n), rel, it, ALU.is_equal)
                    else:
                        rel = rel_l[0:R, 2:4].rearrange("p (t a) -> p t a", a=1).broadcast_to([R, 2, W])
                        it = iota[0:R, :].rearrange("p (a w) -> p a w", a=1).broadcast_to([R, 2, W])
                        ins = dve.tensor_tensor(S_of(n)[0:R, 0:2, :], rel, it, ALU.is_equal)
                    point["S", n] = s_S.inc(ins)

            def gather(upto):
                while made["g"] < min(upto, len(order_g)):
                    u = order_g[made["g"]]
                    made["g"] += 1
                    n, g = seq_g[u], u[1]
                    parts, nt = shape(u)
                    if ("gfree", n - NSLOT) in point:
                        wait(pool, point["gfree", n - NSLOT])
                    for t in range(nt):
                        idx = srcT[:, t, g - DG:g - DG + 1] if g < G else src_l[0:R, t:t + 1]
                        point["gat", n] = s_gat[n % NSLOT].inc(pool.indirect_dma_start(
                            out=g_of(n)[0:parts, t, :], out_offset=None, in_=table0 if k == 0 else tables[k],
                            in_offset=bass.IndirectOffsetOnAxis(ap=idx, axis=0)), 16)

            def load_edges(upto):
                while k == 0 and made["e"] < min(upto, len(uses)):
                    n = made["e"]
                    g = uses[n][1]
                    made["e"] += 1
                    if n >= NEDGE:
                        wait(sp, point["efree", n - NEDGE])
                    if g < G:
                        d = sp.dma_start(ebuf(n % NEDGE)[:, :, 0:F], edge_g[g])
                    else:
                        d = sp.dma_start(ebuf(n % NEDGE)[0:R, 0:2, 0:F], edge_r)
                    point["edg", n] = s_edg[n % NEDGE].inc(d, 16)

            pend = []
            now = want = 0

            def settle(s=None):
                while pend and (s is None or s >= pend[0][0]):
                    pend.pop(0)[1]()

            def add(w, g):
                wait(dve, point["mm", w])
                if ("add", w - 1) in point:
                    wait(dve, point["add", w - 1])
                b = dve.value_load(base[0:1, g:g + 1], min_val=0, max_val=N - 1)
                win = acc[0:rows_a, ds(b, W)]
                point["add", w] = s_add.inc(dve.tensor_tensor(win, win, ps_g[0:rows_a, :], ALU.add))

            def fold_q(p, w):
                wait(dve, p)
                point["fold_q", w] = s_fld.inc(dve.tensor_reduce(
                    qbuf, ps_q.rearrange("p (s f) -> p f s", s=3), X, ALU.add))

            def turn_q(w):
                wait(pe, point["fold_q", w])
                point["mm", w] = s_mm.inc(pe.matmul(ps_g[0:F, :], qbuf, ident[:, :], start=True, stop=True))

            def make_ob(i):
                if i < D:
                    if ("bld", k, i * NT - NT - 1) in point:
                        wait(dve, point["bld", k, i * NT - NT - 1])
                    src_v = hibT[:, i * NT:(i + 1) * NT].rearrange("p (t a) -> p t a", a=1)
                    it = iota16[:, 0:PN].rearrange("p (a b) -> p a b", a=1).broadcast_to([P, NT, PN])
                    point["ob", i] = s_oh.inc(dve.tensor_tensor(ob(i % 2), src_v.broadcast_to([P, NT, PN]), it,
                                                                ALU.is_equal))

            def make_oh(s):
                if s < steps:
                    if s >= NOH:
                        wait(dve, point["bld", k, s - NOH])
                    point["oh", s] = s_oh.inc(dve.tensor_scalar(oh(s % NOH), iota16[:, :], keyT[:, s:s + 1], None,
                                                                ALU.is_equal))

            def step(s):
                i, t = s // NT, s % NT
                if t == 4:
                    make_ob(i + 1)
                make_oh(s + NOH - 1)
                if s - LAG - 1 >= 0 and (s - LAG) % NT == 0:
                    fold((s - LAG - 1) // NT)
                settle(s)
                if s < steps:
                    wait(pe, point["oh", s])
                    if t == 0:
                        wait(pe, point["ob", i])
                    if s >= 2:
                        wait(pe, point["ev", s - 2])
                    for c in range(3):
                        last = pe.matmul(ps_b[s % 2][0:PN, c, 0:KC], ob(i % 2)[:, t, :],
                                         oh(s % NOH)[:, c * KC:(c + 1) * KC], start=True, stop=True)
                    point["bld", k, s] = s_bld.inc(last)
                a = s - LAG
                if 0 <= a < steps:
                    ai, at = a // NT, a % NT
                    if at == 0:
                        wait(pe, point["ev", ai * NT + NT - 1])
                        if ai >= 1:
                            wait(pe, point["fold", ai - 1])
                    for j in range(at * J // NT, (at + 1) * J // NT):
                        last = pe.matmul(ps_v, A[ai % 2][0:PN, j:(P - 1) * J + j + 1:J],
                                         Xs[0:PN, j, :, :], start=(j == 0), stop=(j == J - 1))
                    if at == NT - 1:
                        point["app", ai] = s_app.inc(last)
                if s < steps:
                    wait(act, point["bld", k, s])
                    if t == 0 and i >= 2:
                        wait(act, point["app", i - 2])
                    if t > 0:
                        wait(act, point["ev", s - 1])
                    point["ev", s] = s_ev.inc(act.copy(
                        A[i % 2][0:PN, t * VJ:t * VJ + VP].rearrange("p (c k) -> p c k", c=3),
                        ps_b[s % 2][0:PN, :, 0:KC]))

            def fold(i):
                if i >= D:
                    return
                wait(dve, point["app", i])
                if i >= 2:
                    wait(dve, point["win", i - 2])
                v = vbuf(i % 2)
                point["fold", i] = s_fld.inc(dve.tensor_reduce(
                    v[:, 0:F], ps_v.rearrange("p (s f) -> p f s", s=3), X, ALU.add))
                point["row", i] = s_fld.inc(dve.tensor_scalar(
                    v[:, F:F + W], iota[:, :], rowT[:, i:i + 1], None, ALU.is_equal))

            def use(u):
                nonlocal want
                kind, g = u
                parts, nt = shape(u)
                n_e, w = seq_e[u], seq_w[u]
                settle()
                if u in seq_s:
                    wait(pe, point["S", seq_s[u]])
                S = S_of(seq_s[u]) if u in seq_s else None
                gb = row = eb = None
                if k == 0:
                    eb = ebuf(n_e % NEDGE)
                if kind == "win":
                    wait(pe, point["row", g])
                    row = vbuf(g % 2)
                    if k == 0:
                        wait(pe, point["edg", n_e])
                elif k == 0:
                    wait(dve, point["gat", seq_g[u]], point["edg", n_e])
                    p = s_pre.inc(dve.tensor_tensor(eb[0:parts, 0:nt, 0:F], eb[0:parts, 0:nt, 0:F],
                                                    gbuf(seq_g[u] % NSLOT)[0:parts, 0:nt, :], ALU.add))
                    point["gfree", seq_g[u]] = p
                    wait(pe, p)
                else:
                    wait(pe, point["gat", seq_g[u]])
                if w > 0:
                    wait(pe, point["add", w - 1])
                if kind == "gat" and k > 0:
                    gb = g_of(seq_g[u])
                    for t in range(nt):
                        last = pe.matmul(ps_q, S[0:parts, t, :], gb[0:parts, t, :], start=(t == 0),
                                         stop=(t == nt - 1))
                    p = s_mm.inc(last)
                    pend.append((now + 1, lambda p=p, w=w: fold_q(p, w)))
                    pend.append((now + 2, lambda w=w: turn_q(w)))
                    pend.append((now + 3, lambda w=w, g=g: add(w, g)))
                else:
                    p = s_mm.inc(run_jobs(ps_g, jobs_of(nt, gb, eb), S, parts, row))
                    point["mm", w] = p
                    pend.append((now + 2, lambda w=w, g=g: add(w, g)))
                if kind == "win":
                    point["win", g] = p
                elif k > 0:
                    point["gfree", seq_g[u]] = p
                if u in seq_s:
                    point["Sfree", seq_s[u]] = p
                    want = order_s.index(u) + 1 + NS
                if kind == "gat":
                    gather(order_g.index(u) + 1 + NSLOT)
                if k == 0:
                    point["efree", n_e] = p
                    load_edges(n_e + 1 + NEDGE)
                pend.insert(1, (pend[0][0], lambda n=want: make_S(n)))

            gather(NSLOT)
            load_edges(NEDGE)
            make_ob(0)
            for s in range(NOH - 1):
                make_oh(s)
            make_S(NS)
            for _, _, kind, v in events:
                if kind == "step":
                    step(v)
                    now = v
                else:
                    use((kind, v))
            settle()
            wait(dve, point["add", turn["w"] + len(uses) - 1])
            turn["S"] += len(s_uses)
            turn["g"] += len(order_g)
            turn["w"] += len(uses)

        def take(eng, s, n=1):
            eng.wait_ge(s.h, n)
            eng.sem_clear(s.h)

        def slow_group(k, g, parts, nt):
            rows_a = F + 1 if k == 0 else F
            if parts == P:
                a, b = src_g[ds(g, 1)], dst_g[ds(g, 1)]
                a, b = (v.rearrange("a p t -> (a p) t") for v in (a, b))
                e = edge_g[ds(g, 1)].rearrange("a p t f -> (a p) t f")
            else:
                a, b = src_r, dst_r
                e = edge_r
            sp.dma_start(g_src[0:parts, 0:nt], a).then_inc(t_src.h, 16)
            sp.dma_start(g_dst[0:parts, 0:nt], b).then_inc(t_dst.h, 16)
            if k == 0:
                sp.dma_start(ebuf(0)[0:parts, 0:nt, 0:F], e).then_inc(t_edg.h, 16)
            take(pool, t_src, 16)
            gb, S = (gbuf(0), sbuf(0)) if k == 0 else (gbuf_s(0), sbuf_s(0))
            for t in range(nt):
                pool.indirect_dma_start(
                    out=gb[0:parts, t, :], out_offset=None, in_=table0 if k == 0 else tables[k],
                    in_offset=bass.IndirectOffsetOnAxis(ap=g_src[0:parts, t:t + 1], axis=0)).then_inc(t_gat.h, 16)
            pool.wait_ge(t_gat.h, 16 * nt)
            pool.dma_reset(range(t_gat.h.num, t_gat.h.num + 1))
            pool.sem_clear(t_gat.h)
            pool.sem_inc(t_gd.h, 1)
            take(dve, t_dst, 16)
            dve.tensor_copy(g_cur[0:parts, 0:nt], g_dst[0:parts, 0:nt]).then_inc(t_cur.h, 1)
            take(dve, t_cur)
            take(pe, t_gd)
            if k == 0:
                take(pe, t_edg, 16)
            with nc.Fori(0, (N + W - 1) // W, 1, engines=[pe.engine, dve.engine]) as w:
                cur = g_cur[0:parts, 0:nt].rearrange("p (t a) -> p t a", a=1).broadcast_to([parts, nt, W])
                it = iota[0:parts, :].rearrange("p (a w) -> p a w", a=1).broadcast_to([parts, nt, W])
                dve.tensor_tensor(S[0:parts, 0:nt, :], cur, it, ALU.is_equal).then_inc(t_S.h, 1)
                take(pe, t_S)
                if k == 0:
                    last = run_jobs(ps_g, jobs_of(nt, gb, ebuf(0)), S, parts)
                else:
                    for t in range(nt):
                        for i in range(3):
                            last = pe.matmul(ps_g[0:F, :], gb[0:parts, t, i * F:(i + 1) * F], S[0:parts, t, :],
                                             start=(t == 0 and i == 0), stop=(t == nt - 1 and i == 2))
                last.then_inc(t_mm.h, 1)
                take(dve, t_mm)
                dve.tensor_scalar(g_cur[0:parts, 0:nt], g_cur[0:parts, 0:nt], float(W), None,
                                  ALU.subtract).then_inc(t_cur.h, 1)
                win = acc[0:rows_a, ds(w * W, W)]
                dve.tensor_tensor(win, win, ps_g[0:rows_a, 0:W], ALU.add).then_inc(t_add.h, 1)
                take(dve, t_add)
                take(dve, t_cur)
            dve.sem_inc(t_end.h, 1)
            take(sp, t_end)

        def slow_pass(k):
            if k == 0:
                wait(pool, *(point["gat", n] for n in range(min(NSLOT, G - dense[0]))))
            with nc.Fori(0, G, 1, engines=[e.engine for e in engines]) as g:
                slow_group(k, g, P, NT)
            slow_group(k, None, R, 2)

        p_sq, fv = [], []

        def self_loops(ready):
            freed = {}
            accv = acc[0:F, 0:N].rearrange("f (p j) -> f j p", j=J)
            for c, j0 in enumerate(range(0, J, 4)):
                j1 = min(J, j0 + 4)
                wait(pe, ready[min(NCH - 1, (j1 - 1) // JC)])
                if c >= 2:
                    wait(pe, freed[c - 2])
                for j in range(j0, j1):
                    last = pe.transpose(ps_h[c % 2][0:F, (j - j0) * PN:(j - j0 + 1) * PN],
                                        H[0:PN, j * F:(j + 1) * F], ident[0:PN, 0:PN])
                p = s_p.inc(last)
                got = ps_h[c % 2][0:F, 0:(j1 - j0) * PN].rearrange("f (j p) -> f j p", p=PN)
                if c % 2:
                    wait(dve, p)
                    freed[c] = s_v.inc(dve.tensor_copy(accv[:, j0:j1, :], got))
                else:
                    wait(act, p)
                    freed[c] = s_a.inc(act.copy(accv[:, j0:j1, :], got))
            return [freed[c] for c in list(freed)[-2:]]

        def run_pass(k, acc_ready, ready, did=()):
            if k == 1:
                wait(act, (s_x1.h, s_x1.n))
            p_xs = split_table(k, ready, did)
            tab = (s_tab.h, s_tab.n)
            wait(pool, p_srcT, p_small, tab)
            wait(sp, p_relT)
            if k > 0:
                acc_ready = self_loops(ready)
            for q in range(2):
                V(dve.memset(vbuf(q), 0.0))
            if k == 0:
                for q in range(NEDGE):
                    p = V(dve.memset(ebuf(q)[:, :, F:F + 1], 1.0))
                wait(dve, tab)
            if k == 1:
                p_sq.append(s_a.inc(act.activation(acc[F:F + 1, 0:N], acc[F:F + 1, 0:N], ACT.Sqrt,
                                                   bias=ones[F:F + 1, 0:1])))
            wait(dve, *acc_ready)
            if k == 0:
                first_gathers()
                for eng in engines:
                    wait(eng, p_flag)
                fv.append(nc.values_load(flag[0:1, 0:1], engines=[e.engine for e in engines], min_val=0, max_val=1))
            for q in range(2):
                p = V(dve.memset(A[q][0:PN, NT * VJ:P * J], 0.0))
            wait(pe, p_xs, p)
            wait(act, p)
            with nc.If(fv[0]):
                slow_pass(k)
            with nc.Else():
                fast_pass(k)
            p = s_pass.inc(dve.memset(sc[0:1, 7:8], 0.0))
            wait(dve, p)
            return p

        p_acc = run_pass(0, [p_zero], done)
        wait(sp, p_acc)
        p_d = s_deg.inc(sp.dma_start(deg_dram, acc[F:F + 1, 0:N]), 16)
        wait(sp, p_d)
        p_deg = s_deg.inc(sp.dma_start(dis[0:PN, :], deg_dram.rearrange("a (p j) -> (a p) j", p=PN)), 16)

        def bc_row(t, n):
            return t.rearrange("p (a f) -> p a f", a=1).broadcast_to([PN, n, F])

        wait(sp, p_acc)
        p_xr = s_x1.inc(sp.dma_start(X1[0:PN, :], xv), 16)
        wait(pool, p_xr, p_w)
        p_xb = s_k.inc(pool.tensor_tensor(v3(X1, 0, J), v3(X1, 0, J), bc_row(rows[0:PN, 2, :], J), ALU.add))

        acc_j = acc[:, 0:N].rearrange("f (p j) -> f j p", j=J)
        wait(pe, p_w, p_acc)
        wait(act, p_w)
        wait(dve, p_w)
        hbuf = [H[:, i * 500:(i + 1) * 500] for i in range(3)]
        JH = 4
        assert J % 2 == 0
        chunks = [(j, min(J, j + JH)) for j in range(0, J, JH)]
        hid, up, freed = {}, {}, {}

        def hidden(c):
            j0, j1 = chunks[c]
            n = (j1 - j0) * PN
            if c >= 2:
                wait(pe, hid[c - 2])
            p = s_p.inc(pe.matmul(ps_h[c % 2][:, 0:n], w01[:, :], acc_j[0:F, j0:j1, :], start=True, stop=True))
            wait(act, p)
            if c >= 3:
                wait(act, up[c - 3])
            hid[c] = s_a.inc(act.activation(hbuf[c % 3][:, 0:n], ps_h[c % 2][:, 0:n], ACT.Relu, bias=b01c[:, 0:1]))

        hidden(0)
        for c, (j0, j1) in enumerate(chunks):
            if c + 1 < len(chunks):
                hidden(c + 1)
            ps = ps_t[c // 2 % 2]
            wait(pe, hid[c])
            if c % 2 == 0 and c >= 4:
                wait(pe, freed[c // 2 - 2])
            for j in range(j0, j1):
                o = (c % 2 * JH + j - j0) * F
                last = pe.matmul(ps[0:PN, o:o + F], hbuf[c % 3][:, (j - j0) * PN:(j - j0 + 1) * PN], w02[:, :],
                                 start=True, stop=True)
            up[c] = s_p.inc(last)
            if c % 2 or c == len(chunks) - 1:
                a = chunks[c // 2 * 2][0]
                wait(dve, up[c])
                freed[c // 2] = V(dve.tensor_tensor(v3(C, a, j1), ps[0:PN, 0:(j1 - a) * F].rearrange(
                    "p (j f) -> p j f", f=F), bc_row(rows[0:PN, 0, :], j1 - a), ALU.add))
                V(dve.tensor_reduce(pst[0:PN, c // 2, :],
                                    C[0:PN, a * F:j1 * F].rearrange("p (j f) -> p f j", f=F), X, ALU.add))
        NP = c // 2 + 1

        def node_sum(n, *terms):
            wait(pe, (s_v.h, s_v.n), (s_a.h, s_a.n))
            for i, t in enumerate(terms):
                last = pe.matmul(ps_s[0:PN, 0:n], ones[0:PN, 0:PN], t, start=(i == 0), stop=(i == len(terms) - 1))
            p = s_p.inc(last)
            wait(dve, p)
            return p

        def partials():
            V(dve.tensor_reduce(st[0:PN, 3, :], pst[0:PN, 0:NP, :].rearrange("p c f -> p f c"), X, ALU.add))
            node_sum(F, st[0:PN, 3, :])

        wait(dve, p_deg)
        p = V(dve.tensor_scalar(dis[0:PN, :], dis[0:PN, :], 1.0, None, ALU.add))
        wait(act, p)
        p = s_a.inc(act.activation(dis[0:PN, :], dis[0:PN, :], ACT.Sqrt))
        wait(dve, p)
        V(dve.reciprocal(dis[0:PN, :], dis[0:PN, :]))
        V(dve.tensor_tensor(dis2[0:PN, :], dis[0:PN, :], dis[0:PN, :], ALU.mult))
        partials()
        V(dve.tensor_scalar(st[0:PN, 0, :], ps_s[0:PN, 0:F], 1.0 / N, None, ALU.mult))
        sq = []
        for c in range(NCH):
            j0, j1 = c * JC, (c + 1) * JC
            p = V(dve.tensor_tensor(v3(C, j0, j1), v3(C, j0, j1), bc_row(st[0:PN, 0, :], JC), ALU.subtract))
            wait(act, p)
            sq.append(s_a.inc(act.activation(H[0:PN, j0 * F:j1 * F], C[0:PN, j0 * F:j1 * F], ACT.Square)))
        for c in range(NCH):
            wait(dve, sq[c])
            V(dve.tensor_reduce(pst[0:PN, c, :], H[0:PN, c * JC * F:(c + 1) * JC * F].rearrange(
                "p (j f) -> p f j", f=F), X, ALU.add))
        NP = NCH
        partials()
        p = V(dve.tensor_scalar(st[0:PN, 2, :], ps_s[0:PN, 0:F], 1.0 / N, None, ALU.mult))
        wait(act, p)
        p = s_a.inc(act.activation(st[0:PN, 2, :], st[0:PN, 2, :], ACT.Sqrt, bias=epst[0:PN, 0:1]))
        wait(dve, p)
        V(dve.reciprocal(st[0:PN, 2, :], st[0:PN, 2, :]))
        V(dve.tensor_tensor(st[0:PN, 2, :], st[0:PN, 2, :], rows[0:PN, 1, :], ALU.mult))
        wait(dve, p_xb)
        p_x1 = []
        for c in range(NCH):
            j0, j1 = c * JC, (c + 1) * JC
            V(dve.tensor_tensor(v3(C, j0, j1), v3(C, j0, j1), bc_row(st[0:PN, 2, :], JC), ALU.mult))
            p_x1.append(V(dve.tensor_tensor(v3(X1, j0, j1), v3(X1, j0, j1), v3(C, j0, j1), ALU.add)))
            wait(sp, p_x1[-1])
            s_x1.inc(sp.dma_start(x1_dram.rearrange("(p j) f -> p (j f)", p=PN)[:, j0 * F:j1 * F],
                                  X1[0:PN, j0 * F:j1 * F]), 16)

        V(dve.tensor_scalar(w12a[:, :], w12[0:F, :], GW, None, ALU.mult))
        p_w12 = V(dve.scalar_tensor_tensor(out=w12b[0:F, :], in0=w12[0:F, :], scalar=1.0 - GW, in1=w12a[:, :],
                                           op0=ALU.mult, op1=ALU.add))
        wait(pe, p_w12)

        done = norm_table(1, p_x1, dis)
        p_acc = run_pass(1, None, done)

        def by_node(wt, use):
            freed = {}
            wait(pe, p_acc, *p_sq)
            for c, j0 in enumerate(range(0, J, 8)):
                j1 = min(J, j0 + 8)
                ps = ps_t[c % 2]
                if c >= 2:
                    wait(pe, freed[c - 2])
                for j in range(j0, j1):
                    last = pe.matmul(ps[0:PN, (j - j0) * F:(j - j0 + 1) * F], acc_j[0:F + 1, j, :],
                                     wt[:, :], start=True, stop=True)
                p = s_p.inc(last)
                wait(dve, p)
                freed[c] = use(c, j0, j1, ps[0:PN, 0:(j1 - j0) * F].rearrange("p (j f) -> p j f", f=F))

        queued, did, p_c = [], [], {}

        def to_table(c, j0, j1, ps):
            p = V(dve.scalar_tensor_tensor(out=v3(H, j0, j1), in0=ps, scalar=0.0, in1=bc_f(dis2, j0, j1),
                                           op0=ALU.max, op1=ALU.mult))
            queued.extend((d, i) for d in range(NCH) for i in range(3) if j0 < (d + 1) * JC <= j1)
            for d, i in queued:
                if d not in p_c:
                    p_c[d] = p
            if len(did) < len(queued):
                d, i = queued[len(did)]
                split_part(2, p_c, d, i)
                did.append((d, i))
            return p

        by_node(w11, to_table)
        p_acc = run_pass(2, None, [p_c[c] for c in range(NCH)], did)
        wait(sp, p_acc)
        p_xr = s_x1.inc(sp.dma_start(X1[0:PN, :], x1_dram.rearrange("(p j) f -> p (j f)", p=PN)), 16)

        def to_rows(c, j0, j1, ps):
            p = V(dve.scalar_tensor_tensor(out=v3(C, j0, j1), in0=ps, scalar=0.0, in1=bc_f(dis, j0, j1),
                                           op0=ALU.max, op1=ALU.mult))
            V(dve.tensor_reduce(mm[0:PN, c:c + 1], C[0:PN, j0 * F:j1 * F], X, ALU.add))
            return p

        by_node(w12b, to_rows)
        NC = (J + 7) // 8
        assert NC <= 16
        V(dve.tensor_reduce(sc[0:PN, 0:1], mm[0:PN, 0:NC], X, ALU.add))
        node_sum(1, sc[0:PN, 0:1])
        p = V(dve.tensor_scalar(sc[0:PN, 1:2], ps_s[0:PN, 0:1], -1.0 / (N * F), None, ALU.mult))
        wait(act, p)
        half = JF // 2
        s_a.inc(act.activation(H[0:PN, 0:half], C[0:PN, 0:half], ACT.Square, bias=sc[0:PN, 1:2],
                               accum_out=sc[0:PN, 2:3]))
        V(dve.tensor_scalar(H[0:PN, half:JF], C[0:PN, half:JF], sc[0:PN, 1:2], None, ALU.add))
        V(dve.tensor_tensor_reduce(H[0:PN, half:JF], H[0:PN, half:JF], H[0:PN, half:JF], 1.0, 0.0, ALU.mult,
                                   ALU.add, sc[0:PN, 4:5]))
        node_sum(1, sc[0:PN, 2:3], sc[0:PN, 4:5])
        p = V(dve.tensor_scalar(sc[0:PN, 3:4], ps_s[0:PN, 0:1], 1.0 / (N * F), None, ALU.mult))
        wait(act, p)
        p = s_a.inc(act.activation(sc[0:PN, 3:4], sc[0:PN, 3:4], ACT.Sqrt, bias=epst[0:PN, 0:1]))
        wait(dve, p)
        V(dve.reciprocal(sc[0:PN, 3:4], sc[0:PN, 3:4]))
        V(dve.tensor_tensor(sc[0:PN, 3:4], sc[0:PN, 3:4], lnwb[0:PN, 0:1], ALU.mult))
        p = V(dve.scalar_tensor_tensor(out=sc[0:PN, 5:6], in0=sc[0:PN, 1:2], scalar=sc[0:PN, 3:4],
                                       in1=lnwb[0:PN, 1:2], op0=ALU.mult, op1=ALU.add))
        outv = out.rearrange("(p j) f -> p (j f)", p=PN)
        wait(act, p)
        wait(dve, p_xr)
        for c in range(NCH):
            a, b = c * JC * F, (c + 1) * JC * F
            p = s_a.inc(act.activation(C[0:PN, a:b], C[0:PN, a:b], ACT.Identity, bias=sc[0:PN, 5:6],
                                       scale=sc[0:PN, 3:4]))
            wait(dve, p)
            p = V(dve.tensor_tensor(X1[0:PN, a:b], X1[0:PN, a:b], C[0:PN, a:b], ALU.add))
            wait(sp, p)
            s_out.inc(sp.dma_start(outv[:, a:b], X1[0:PN, a:b]), 16)
        sp.wait_ge(s_out.h, s_out.n)
        sp.wait_ge(s_tab.h, s_tab.n)
        sp.wait_ge(s_deg.h, s_deg.n)


_INS = ['x', 'src', 'dst', 'edge_attr_64', 'L0_gnn_W1', 'L0_gnn_b1', 'L0_gnn_W2', 'L0_gnn_b2',
        'L0_gnn_bn_gamma', 'L0_gnn_bn_beta', 'L1_gnn_W1', 'L1_gnn_b1', 'L1_gnn_W2', 'L1_gnn_b2',
        'L1_gnn_ln_w', 'L1_gnn_ln_b']


def kernel(**inputs):
    import numpy as _np
    import concourse.bacc as _bacc
    from concourse import mybir as _mybir
    from concourse.bass_utils import run_bass_kernel_spmd as _run

    nc = _bacc.Bacc("TRN2", target_bir_lowering=False, num_devices=1)
    arrays, args = {}, []
    for name in _INS:
        a = _np.ascontiguousarray(inputs[name])
        arrays[f"in_{name}_dram"] = a
        args.append(nc.dram_tensor(f"in_{name}_dram", a.shape, _mybir.dt.from_np(a.dtype), kind="ExternalInput").ap())
    out = nc.dram_tensor("out_0_dram", inputs['x'].shape, _mybir.dt.float32, kind="ExternalOutput").ap()
    bass_gnn_preln_kernel(nc, *args, out)
    r = _run(nc, [arrays], core_ids=[0])
    return r.results[0]["out_0_dram"]
```
